# Optimizing a Trainium2 kernel written in Bass

```python
import numpy as np
import jax
import jax.numpy as jnp

def _softmax(x, axis=-1):
    return jax.nn.softmax(x, axis=axis)

def _gelu(x):
    return jax.nn.gelu(x, approximate=True)

def _silu(x):
    return jax.nn.silu(x)

def _sigmoid(x):
    return jax.nn.sigmoid(x)

def _layernorm(x, axis=-1, eps=1e-05):
    m = jnp.mean(x, axis=axis, keepdims=True)
    v = jnp.var(x, axis=axis, keepdims=True)
    return (x - m) / jnp.sqrt(v + eps)

def _scatter_add(tgt, idx, src, axis=0):
    return tgt.at[idx].add(src)

def _segment_sum(src, seg, n):
    return jax.ops.segment_sum(src, seg, n)
kernel_name = 'mk_macaron_d1_jaxref_r8_64c3c9'

def setup_inputs(seed: int=0):
    np.random.seed(seed)
    _w = jnp.asarray

    def _L0_attn_setup():
        import jax, jax.numpy as jnp
        import numpy as np
        import math
        DIM = 128
        HEADS = 16
        DIM_K = DIM // HEADS
        SEQ = 256

        def _rope_tables(seq_len, dim):
            pos = jnp.arange(seq_len, dtype=jnp.float32)[:, None]
            freqs = jnp.exp(jnp.arange(0, dim, 2, dtype=jnp.float32) * (-math.log(10000.0) / dim))
            ang = pos * freqs
            return (jnp.cos(ang), jnp.sin(ang))

        def _apply_rope(x, cos, sin):
            even = x[..., ::2]
            odd = x[..., 1::2]
            return jnp.concatenate([even * cos - odd * sin, even * sin + odd * cos], axis=-1)
        key = jax.random.key(seed)
        ks = jax.random.split(key, 6)
        B, S, D = (2, SEQ, DIM)
        scale = 1.0 / math.sqrt(D)
        return {'x': jax.random.normal(ks[0], (B, S, D), dtype=jnp.float32), 'wq': jax.random.normal(ks[1], (D, D), dtype=jnp.float32) * scale, 'wk': jax.random.normal(ks[2], (D, D), dtype=jnp.float32) * scale, 'wv': jax.random.normal(ks[3], (D, D), dtype=jnp.float32) * scale, 'wo_w': jax.random.normal(ks[4], (D, D), dtype=jnp.float32) * scale, 'wo_b': jax.random.normal(ks[5], (D,), dtype=jnp.float32) * 0.01}
    _L0_attn_in = _L0_attn_setup()

    def _L0_ffn_setup():
        import jax, jax.numpy as jnp
        import numpy as np
        E = 16
        K = 4
        B, S, H, I = (4, 128, 128, 256)
        key = jax.random.key(seed)
        k0, k1, k2, k3 = jax.random.split(key, 4)
        scale = 0.02
        return {'hidden_states': jax.random.normal(k0, (B, S, H), jnp.float32), 'router_w': jax.random.normal(k1, (H, E), jnp.float32) * scale, 'router_b': jnp.zeros((E,), jnp.float32), 'w1': jax.random.normal(k2, (E, H, I), jnp.float32) * scale, 'b1': jnp.zeros((E, I), jnp.float32), 'w2': jax.random.normal(k3, (E, I, H), jnp.float32) * scale, 'b2': jnp.zeros((E, H), jnp.float32)}
    _L0_ffn_in = _L0_ffn_setup()
    _d = {'L0_attn_x': _L0_attn_in['x'], 'L0_attn_wq': _L0_attn_in['wq'], 'L0_attn_wk': _L0_attn_in['wk'], 'L0_attn_wv': _L0_attn_in['wv'], 'L0_attn_wo_w': _L0_attn_in['wo_w'], 'L0_attn_wo_b': _L0_attn_in['wo_b'], 'L0_ffn_router_w': _L0_ffn_in['router_w'], 'L0_ffn_router_b': _L0_ffn_in['router_b'], 'L0_ffn_w1': _L0_ffn_in['w1'], 'L0_ffn_b1': _L0_ffn_in['b1'], 'L0_ffn_w2': _L0_ffn_in['w2'], 'L0_ffn_b2': _L0_ffn_in['b2']}
    _x0 = _d['L0_attn_x']
    _d['L0_attn_x'] = jax.random.normal(jax.random.fold_in(jax.random.key(seed), 1), (1, 2048, 128), dtype=_x0.dtype)
    del _x0
    return _d

def reference(L0_attn_x, L0_attn_wq, L0_attn_wk, L0_attn_wv, L0_attn_wo_w, L0_attn_wo_b, L0_ffn_router_w, L0_ffn_router_b, L0_ffn_w1, L0_ffn_b1, L0_ffn_w2, L0_ffn_b2):

    def _L0_attn_ref(x, wq, wk, wv, wo_w, wo_b):
        import jax, jax.numpy as jnp
        import numpy as np
        import math
        DIM = 128
        HEADS = 16
        DIM_K = DIM // HEADS
        SEQ = 256

        def _rope_tables(seq_len, dim):
            pos = jnp.arange(seq_len, dtype=jnp.float32)[:, None]
            freqs = jnp.exp(jnp.arange(0, dim, 2, dtype=jnp.float32) * (-math.log(10000.0) / dim))
            ang = pos * freqs
            return (jnp.cos(ang), jnp.sin(ang))

        def _apply_rope(x, cos, sin):
            even = x[..., ::2]
            odd = x[..., 1::2]
            return jnp.concatenate([even * cos - odd * sin, even * sin + odd * cos], axis=-1)
        B, S, D = x.shape
        cos, sin = _rope_tables(S, D)
        Q = _apply_rope(jnp.einsum('bsd,ed->bse', x, wq), cos, sin)
        K = _apply_rope(jnp.einsum('bsd,ed->bse', x, wk), cos, sin)
        V = jnp.einsum('bsd,ed->bse', x, wv)
        Q = Q.reshape(B, S, HEADS, DIM_K).transpose(0, 2, 1, 3)
        K = K.reshape(B, S, HEADS, DIM_K).transpose(0, 2, 1, 3)
        V = V.reshape(B, S, HEADS, DIM_K).transpose(0, 2, 1, 3)
        scores = jnp.einsum('bhqd,bhkd->bhqk', Q, K) / math.sqrt(DIM_K)
        weights = jax.nn.softmax(scores, axis=-1)
        out = jnp.einsum('bhqk,bhkd->bhqd', weights, V)
        out = out.transpose(0, 2, 1, 3).reshape(B, S, D)
        return jnp.einsum('bsd,ed->bse', out, wo_w) + wo_b

    def _L0_ffn_ref(hidden_states, router_w, router_b, w1, b1, w2, b2):
        import jax, jax.numpy as jnp
        import numpy as np
        E = 16
        K = 4
        B, S, H, I = (4, 128, 128, 256)
        b, s, h = hidden_states.shape
        logits = hidden_states @ router_w + router_b
        probs = jax.nn.softmax(logits, axis=-1)
        topw, topi = jax.lax.top_k(probs, K)
        topw = topw / jnp.sum(topw, axis=-1, keepdims=True)
        combine = jnp.sum(jax.nn.one_hot(topi, E, dtype=hidden_states.dtype) * topw[..., None], axis=2)
        x = hidden_states.reshape(b * s, h)
        c = combine.reshape(b * s, E)

        def body(acc, expert):
            w1e, b1e, w2e, b2e, ce = expert
            hmid = jax.nn.gelu(x @ w1e + b1e, approximate=False)
            return (acc + (hmid @ w2e + b2e) * ce[:, None], None)
        out, _ = jax.lax.scan(body, jnp.zeros_like(x), (w1, b1, w2, b2, c.T))
        return out.reshape(b, s, h)
    x = L0_attn_x
    x = x + 0.5 * _L0_ffn_ref(_layernorm(x, axis=-1), L0_ffn_router_w, L0_ffn_router_b, L0_ffn_w1, L0_ffn_b1, L0_ffn_w2, L0_ffn_b2)
    x = x + _L0_attn_ref(_layernorm(x, axis=-1), L0_attn_wq, L0_attn_wk, L0_attn_wv, L0_attn_wo_w, L0_attn_wo_b)
    x = x + 0.5 * _L0_ffn_ref(_layernorm(x, axis=-1), L0_ffn_router_w, L0_ffn_router_b, L0_ffn_w1, L0_ffn_b1, L0_ffn_w2, L0_ffn_b2)
    return x

_drawn_inputs = setup_inputs


def setup_inputs(seed=0):
    import zlib

    import numpy as np

    out = dict(_drawn_inputs(seed))
    spreads = {'L0_ffn_router_b': (0.0, 0.1), 'L0_ffn_b1': (0.0, 0.8), 'L0_ffn_b2': (0.0, 0.1)}
    factors = {'L0_attn_wo_b': 4.698, 'L0_ffn_w1': 2.998, 'L0_ffn_w2': 2.694}
    for name, (base, spread) in spreads.items():
        noise = np.random.default_rng([zlib.crc32(name.encode()), seed]).standard_normal(out[name].shape)
        drawn = base * np.exp(spread * noise) if base else spread * noise
        out[name] = jnp.asarray(drawn.astype(out[name].dtype))
    for name, factor in factors.items():
        out[name] = (out[name] * factor).astype(out[name].dtype)
    return out
```

```python
from contextlib import ExitStack

import concourse.bass as bass
from concourse import mybir

F32 = mybir.dt.float32
F32R = mybir.dt.float32r
ALU = mybir.AluOpType
ACT = mybir.ActivationFunctionType
AX_X = mybir.AxisListType.X

P = 128
SEQ = 2048
DIM = 128
NT = SEQ // P
BLK = 512
NB = SEQ // BLK
TPB = BLK // P
E = 16
TOPK = 4
INNER = 256
HALVES = INNER // P
UNITS = E * HALVES
HEADS = 16
DK = DIM // HEADS
HG = 4
NG = HEADS // HG
QUAD = 32
ROW_M = 3 * DK
VW = DK + 1
EPS = 1e-5
SCALE = DK ** -0.5


def f32(ap):
    return ap.bitcast(F32)


class Chain:

    def __init__(self, eng, sem):
        self.eng, self.sem, self.n = eng, sem, 0

    def link(self, ins):
        ins.then_inc(self.sem, 1)
        self.n += 1
        self.eng.wait_ge(self.sem, self.n)


def blocks_loop(eng, body):
    with eng.Fori(0, NB - 1) as it:
        body(it, False)
    body(NB - 1, True)


def layernorm_stats(nc, dve, chain, x_tok, st, mv, var, rstd, sem_var, sem_sqrt, small):
    for t in range(NT):
        last = nc.vector.bn_stats(st[:, t, :], x_tok[:, t, :])
    chain.link(last)
    for t in range(NT):
        last = nc.vector.bn_aggr(mv[:, t, :], st[:, t, :])
    chain.link(last)
    nc.vector.tensor_scalar(var[:], mv[:, :, 1], EPS, None, ALU.add).then_inc(sem_var, 1)
    dve.wait_ge(sem_sqrt, 1)
    chain.link(nc.vector.reciprocal(rstd[:], small[:, 0, :]))
    chain.link(nc.vector.tensor_tensor(small[:, 1, :], rstd[:], rstd[:], ALU.mult))
    chain.link(nc.vector.tensor_tensor(small[:, 2, :], small[:, 1, :], var[:], ALU.mult))
    chain.link(nc.vector.tensor_scalar(small[:, 3, :], small[:, 2, :], -0.5, 1.5, ALU.mult, ALU.add))
    chain.link(nc.vector.tensor_tensor(small[:, 4, :], small[:, 3, :], rstd[:], ALU.mult))


def ffn_phase(nc, nm, dram, consts, x_tok, weights, first):
    w1h, w1l, w2h, w2l, b2h, b2l, rwh, rwl = weights
    ident, onehot, b1, rb = consts["ident"], consts["onehot"], consts["b1"], consts["rb"]
    with ExitStack() as ctx:
        def sb(name, shape, dt=F32):
            return ctx.enter_context(nc.sbuf_tensor(nm + name, shape, dt))

        def pb(name, shape):
            return ctx.enter_context(nc.psum_tensor(nm + name + "_ps", shape, F32))

        def sem(name):
            return ctx.enter_context(nc.semaphore(nm + name))

        hh = sb("hh", [P, SEQ], F32R)
        hl = sb("hl", [P, SEQ], F32R)
        h_tok = sb("h_tok", [P, NT, DIM])
        st, mv = sb("st", [P, NT, 6]), sb("mv", [P, NT, 2])
        var, rstd, small = sb("var", [P, NT]), sb("rstd", [P, NT]), sb("small", [P, 5, NT])
        lg, ex, gt, eq = (sb(n, [P, NT, E]) for n in ("lg", "ex", "gt", "eq"))
        cs = sb("cs", [P, 2, NT, 2 * E])
        top8 = sb("top8", [P, NT, 8])
        need, tot, rtot = sb("need", [P, NT]), sb("tot", [P, NT]), sb("rtot", [P, NT])
        ct = sb("ct", [P, NT, E])
        c2 = sb("c2", [P, NT, P])
        c2T = sb("c2T", [P, SEQ], F32R)
        g = sb("g", [P, 2, BLK])
        gc = sb("gc", [P, 4, BLK])
        gh, gl = sb("gh", [P, 4, BLK], F32R), sb("gl", [P, 4, BLK], F32R)
        yT = sb("yT", [P, SEQ])
        mid = pb("mid", [P, 4, BLK])
        cb = pb("cb", [P, 2, BLK])
        acc = pb("acc", [P, BLK])
        tp = pb("tp", [P, TPB, P])

        if first:
            w1f, w2f = sb("w1f", [P, E * INNER]), sb("w2f", [P, E * INNER])
            b2f, rwf = sb("b2f", [P, DIM]), sb("rwf", [P, E])
            ohf = gc[:].rearrange("p a b -> p (a b)")
            s_x, s_small, s_w1, s_w2 = sem("x"), sem("small_in"), sem("w1_in"), sem("w2_in")
            s_hi, s_wready = sem("weights_hi"), sem("weights_lo")
        s_out = sem("out")
        s_dve, s_act = sem("dve_chain"), sem("act_chain")
        s_var, s_sqrt, s_h = sem("var"), sem("sqrt"), sem("h_tok")
        s_tp, s_hh, s_hl = sem("h_transposed"), sem("hh"), sem("hl")
        s_lg, s_lm, s_ex, s_c2 = sem("logits"), sem("logits_less_max"), sem("exp"), sem("c2")
        s_ctp, s_c2T = sem("c2_transposed"), sem("c2T")
        s_mid, s_gelu, s_cb, s_gc = sem("mid"), sem("gelu"), sem("cb"), sem("gc")
        s_ghi, s_glo, s_down, s_acc = sem("gh"), sem("gl"), sem("down"), sem("acc_copied")
        s_yt, s_xn = sem("y_transposed"), sem("x_new")
        SLOTS = 4
        block = ctx.enter_context(nc.Block())
        w1fv, w2fv = None, None
        CH = 1024
        NCH = E * INNER // CH

        @block.sync
        def _(sp):
            if first:
                xv = dram["x"].rearrange("(t p) d -> p t d", p=P)
                for b in range(NB):
                    sp.dma_start(x_tok[:, b * TPB:(b + 1) * TPB, :], xv[:, b * TPB:(b + 1) * TPB, :]).then_inc(s_x, 16)
                for dst, src in ((ident[:], "ident"), (ohf, "onehot"), (b1[:], "b1"), (rb[:], "rb"),
                                 (b2f[:], "b2"), (rwf[:], "rw")):
                    sp.dma_start(dst, dram[src]).then_inc(s_small, 16)
                epc = CH // INNER
                for c in range(NCH):
                    sp.dma_start(w1f[:, c * CH:(c + 1) * CH].rearrange("p (e i) -> p e i", i=INNER),
                                 dram["w1"][c * epc:(c + 1) * epc].rearrange("e p i -> p e i")).then_inc(s_w1, 16)
                for c in range(NCH):
                    sp.dma_start(w2f[:, c * CH:(c + 1) * CH].rearrange("p (e t h) -> p e t h", t=HALVES, h=DIM),
                                 dram["w2"][c * epc:(c + 1) * epc].rearrange("e (t p) h -> p e t h", p=P)).then_inc(s_w2, 16)
            else:
                ov = dram["out"].rearrange("(t p) d -> p t d", p=P)
                for b in range(NB):
                    sp.wait_ge(s_xn, b + 1)
                    sp.dma_start(ov[:, b * TPB:(b + 1) * TPB, :], x_tok[:, b * TPB:(b + 1) * TPB, :]).then_inc(s_out, 16)
                sp.wait_ge(s_out, 16 * NB)

        @block.scalar
        def _(act):
            act.wait_ge(s_var, 1)
            nc.scalar.activation(small[:, 0, :], var[:], ACT.Sqrt).then_inc(s_sqrt, 1)
            for b in range(NB):
                act.wait_ge(s_tp, b + 1)
                nc.scalar.copy(hh[:, b * BLK:(b + 1) * BLK], mid[:, b, :]).then_inc(s_hh, 1)
            if first:
                act.wait_ge(s_small, 16 * 6)
                for dst, src in ((rwh, rwf), (b2h, b2f)):
                    nc.scalar.copy(dst[:], src[:]).then_inc(s_hi, 1)
                nc.scalar.copy(onehot[:], ohf).then_inc(s_hi, 1)
                nc.scalar.copy(consts["identr"][:], ident[:]).then_inc(s_hi, 1)
                for c in range(NCH):
                    act.wait_ge(s_w1, 16 * NCH)
                    nc.scalar.copy(w1h[:, c * CH:(c + 1) * CH], w1f[:, c * CH:(c + 1) * CH]).then_inc(s_hi, 1)
                for c in range(NCH):
                    act.wait_ge(s_w2, 16 * NCH)
                    nc.scalar.copy(w2h[:, c * CH:(c + 1) * CH], w2f[:, c * CH:(c + 1) * CH]).then_inc(s_hi, 1)
            act.wait_ge(s_lm, 1)
            nc.scalar.activation(ex[:], lg[:], ACT.Exp).then_inc(s_ex, 1)
            for b in range(NB):
                act.wait_ge(s_ctp, b + 1)
                nc.scalar.copy(c2T[:, b * BLK:(b + 1) * BLK], cb[:, b % 2, :]).then_inc(s_c2T, 1)

            act.sem_inc(s_gelu, SLOTS)
            act.sem_inc(s_acc, 1)

            def gelu(it, u):
                U, e = it * UNITS + u, u % UNITS
                act.wait_ge(s_mid, U + 1)
                nc.scalar.activation(g[:, u % 2, :], mid[:, u % 4, :], ACT.Gelu,
                                     bias=b1[:, e:e + 1]).then_inc(s_gelu, 1)

            def body(it, last):
                for u in range(UNITS):
                    if not (last and u == UNITS - 1):
                        gelu(it, u + 1)
                    U = it * UNITS + u
                    act.wait_ge(s_gc, U + 1)
                    act.wait_ge(s_down, U + 1)
                    nc.scalar.copy(gh[:, u % 4, :], gc[:, u % 4, :]).then_inc(s_ghi, 1)
                act.wait_ge(s_down, SLOTS + (it + 1) * UNITS)
                nc.scalar.copy(yT[:, bass.ts(it, BLK)], acc[:]).then_inc(s_acc, 1)

            gelu(0, 0)
            blocks_loop(act, body)

        @block.vector
        def _(dve):
            ch = Chain(dve, s_dve)
            if first:
                dve.wait_ge(s_x, 16 * NB)
            layernorm_stats(nc, dve, ch, x_tok, st, mv, var, rstd, s_var, s_sqrt, small)
            for t in range(NT):
                nc.vector.tensor_scalar(h_tok[:, t, :], x_tok[:, t, :], mv[:, t, 0:1], small[:, 4, t:t + 1],
                                        ALU.subtract, ALU.mult).then_inc(s_h, 1)
            for b in range(NB):
                dve.wait_ge(s_hh, b + 1)
                s = slice(b * BLK, (b + 1) * BLK)
                nc.vector.tensor_tensor(hl[:, s], mid[:, b, :], f32(hh[:, s]), ALU.subtract).then_inc(s_hl, 1)
            if first:
                n_hi = 0
                for dst, src, hi in ((rwl, rwf, rwh), (b2l, b2f, b2h)):
                    n_hi += 1
                    dve.wait_ge(s_hi, n_hi)
                    nc.vector.tensor_tensor(dst[:], src[:], f32(hi[:]), ALU.subtract).then_inc(s_wready, 1)
                n_hi += 2
                for dst, src, hi in ((w1l, w1f, w1h), (w2l, w2f, w2h)):
                    for c in range(NCH):
                        n_hi += 1
                        s = slice(c * CH, (c + 1) * CH)
                        dve.wait_ge(s_hi, n_hi)
                        nc.vector.tensor_tensor(dst[:, s], src[:, s], f32(hi[:, s]), ALU.subtract).then_inc(s_wready, 1)
            nc.vector.memset(cs[:], 0.0)
            ch.link(nc.vector.memset(c2[:], 0.0))
            dve.wait_ge(s_lg, 1)
            lgp = acc[:, 0:NT * E].rearrange("p (t e) -> p t e", e=E)
            ch.link(nc.vector.tensor_tensor(lg[:], lgp, rb[:].unsqueeze(1).to_broadcast([P, NT, E]), ALU.add))
            for t in range(NT):
                last = nc.vector.max(top8[:, t, :], lg[:, t, :])
            ch.link(last)
            thr = top8[:, :, TOPK - 1:TOPK].to_broadcast([P, NT, E])
            ch.link(nc.vector.tensor_tensor(gt[:], lg[:], thr, ALU.is_gt))
            ch.link(nc.vector.tensor_tensor(eq[:], lg[:], thr, ALU.is_equal))
            ch.link(nc.vector.tensor_copy(cs[:, 0, :, E:], eq[:]))
            nc.vector.tensor_tensor(lg[:], lg[:], top8[:, :, 0:1].to_broadcast([P, NT, E]),
                                    ALU.subtract).then_inc(s_lm, 1)
            step, cur = 1, 0
            while step < E:
                ch.link(nc.vector.tensor_tensor(cs[:, 1 - cur, :, E:], cs[:, cur, :, E:],
                                                cs[:, cur, :, E - step:2 * E - step], ALU.add))
                step, cur = 2 * step, 1 - cur
            ch.link(nc.vector.tensor_reduce(tot[:], gt[:], AX_X, ALU.add))
            ch.link(nc.vector.tensor_scalar(need[:], tot[:], -1.0, float(TOPK), ALU.mult, ALU.add))
            ch.link(nc.vector.tensor_tensor(ct[:], cs[:, cur, :, E:],
                                            need[:].unsqueeze(2).to_broadcast([P, NT, E]), ALU.is_le))
            ch.link(nc.vector.tensor_tensor(eq[:], eq[:], ct[:], ALU.mult))
            ch.link(nc.vector.tensor_tensor(gt[:], gt[:], eq[:], ALU.add))
            dve.wait_ge(s_ex, 1)
            ch.link(nc.vector.tensor_tensor(ex[:], ex[:], gt[:], ALU.mult))
            ch.link(nc.vector.tensor_reduce(tot[:], ex[:], AX_X, ALU.add))
            ch.link(nc.vector.reciprocal(rtot[:], tot[:]))
            ch.link(nc.vector.tensor_scalar(rtot[:], rtot[:], 0.5, None, ALU.mult))
            ch.link(nc.vector.tensor_tensor(ct[:], ex[:], rtot[:].unsqueeze(2).to_broadcast([P, NT, E]), ALU.mult))
            ch.link(nc.vector.tensor_copy(c2[:, :, 0:E].bitcast(F32R), ct[:]))
            nc.vector.tensor_tensor(c2[:, :, E:2 * E].bitcast(F32R), ct[:], c2[:, :, 0:E], ALU.subtract).then_inc(s_c2, 1)

            dve.sem_inc(s_glo, SLOTS)

            def gate(it, u):
                U = it * UNITS + u
                dve.wait_ge(s_gelu, U + 1 + SLOTS)
                dve.wait_ge(s_cb, it * E + u // HALVES + 1)
                dve.wait_ge(s_glo, U + 1)
                nc.vector.tensor_tensor(gc[:, u % 4, :], g[:, u % 2, :], cb[:, u // HALVES % 2, :],
                                        ALU.mult).then_inc(s_gc, 1)

            def body(it, last):
                for u in range(UNITS):
                    if not (last and u == UNITS - 1):
                        gate(it, u + 1)
                    U = it * UNITS + u
                    dve.wait_ge(s_ghi, U + 1)
                    dve.wait_ge(s_down, U + 1)
                    nc.vector.tensor_tensor(gl[:, u % 4, :], gc[:, u % 4, :], f32(gh[:, u % 4, :]),
                                            ALU.subtract).then_inc(s_glo, 1)

            gate(0, 0)
            blocks_loop(dve, body)
            for b in range(NB):
                dve.wait_ge(s_yt, b + 1)
                xs = x_tok[:, b * TPB:(b + 1) * TPB, :]
                nc.vector.tensor_tensor(xs, xs, mid[:, b, :].rearrange("p (t d) -> p t d", d=DIM),
                                        ALU.add).then_inc(s_xn, 1)

        @block.tensor
        def _(pe):
            if first:
                pe.wait_ge(s_small, 16 * 6)
            for t in range(NT):
                pe.wait_ge(s_h, t + 1)
                mm = nc.tensor.transpose(mid[:, t // TPB, (t % TPB) * P:(t % TPB + 1) * P], h_tok[:, t, :], ident[:])
                if t % TPB == TPB - 1:
                    mm.then_inc(s_tp, 1)
            if first:
                pe.wait_ge(s_wready, 2)
            pe.wait_ge(s_hl, NB)
            for t in range(NT):
                ts, pairs = slice(t * P, (t + 1) * P), ((hh, rwh), (hh, rwl), (hl, rwh), (hl, rwl))
                for n, (a, b) in enumerate(pairs):
                    mm = nc.tensor.matmul(acc[:, t * E:(t + 1) * E], a[:, ts], b[:], start=(n == 0), stop=(n == 3))
            mm.then_inc(s_lg, 1)

            def mids(it, u):
                e, half = u % UNITS // HALVES, u % HALVES
                U = it * UNITS + u
                if not (isinstance(U, int) and U < 4):
                    pe.wait_ge(s_gelu, U + 1)
                w = slice(e * INNER + half * P, e * INNER + (half + 1) * P)
                if isinstance(it, int):
                    ts = slice(U // UNITS * BLK, (U // UNITS + 1) * BLK)
                else:
                    ts = bass.ts(it + u // UNITS, BLK)
                for n, (a, b) in enumerate(((w1h, hh), (w1h, hl), (w1l, hh))):
                    mm = nc.tensor.matmul(mid[:, u % 4, :], a[:, w], b[:, ts], start=(n == 0), stop=(n == 2))
                mm.then_inc(s_mid, 1)

            def spread(it, e):
                if isinstance(it, int):
                    G = it * E + e
                    if G >= 2:
                        pe.wait_ge(s_gc, 2 * G - 2)
                    ts = slice(G // E * BLK, (G // E + 1) * BLK)
                else:
                    pe.wait_ge(s_gc, it * UNITS + 2 * e - 2)
                    ts = bass.ts(it + e // E, BLK)
                nc.tensor.matmul(cb[:, e % 2, :], onehot[:, e % E * P:(e % E + 1) * P], c2T[:, ts],
                                 start=True, stop=True).then_inc(s_cb, 1)

            if first:
                pe.wait_ge(s_wready, 2 + NCH)
            for u in range(3):
                mids(0, u)
            pe.wait_ge(s_c2, 1)
            for b in range(NB):
                if b >= 2:
                    pe.wait_ge(s_c2T, b - 1)
                for t in range(TPB):
                    mm = nc.tensor.transpose(cb[:, b % 2, t * P:(t + 1) * P], c2[:, b * TPB + t, :], ident[:])
                mm.then_inc(s_ctp, 1)
            pe.wait_ge(s_c2T, NB)
            spread(0, 0)
            spread(0, 1)
            if first:
                pe.wait_ge(s_wready, 2 + 2 * NCH)
            pe.sem_inc(s_down, SLOTS)
            LEAD = 3

            def body(it, last):
                for u in range(UNITS):
                    if not (last and u + LEAD >= UNITS):
                        mids(it, u + LEAD)
                        if (u + LEAD) % HALVES == 0:
                            spread(it, (u + LEAD) // HALVES)
                    U = it * UNITS + u
                    e, half = u // HALVES, u % HALVES
                    if u == 0:
                        pe.wait_ge(s_acc, it + 1)
                        for n, b in enumerate((b2h, b2l)):
                            nc.tensor.matmul(acc[:], b[:], c2T[:, bass.ts(it, BLK)], start=(n == 0), stop=False)
                    pe.wait_ge(s_glo, U + 1 + SLOTS)
                    w = slice((e * HALVES + half) * DIM, (e * HALVES + half + 1) * DIM)
                    for n, (a, b) in enumerate(((w2h, gh), (w2h, gl), (w2l, gh))):
                        mm = nc.tensor.matmul(acc[:], a[:, w], b[:, u % 4, :], start=False,
                                              stop=(u == UNITS - 1 and n == 2))
                    mm.then_inc(s_down, 1)

            blocks_loop(pe, body)
            pe.wait_ge(s_acc, NB + 1)
            for t in range(NT):
                mm = nc.tensor.transpose(mid[:, t // TPB, (t % TPB) * P:(t % TPB + 1) * P],
                                         yT[:, t * P:(t + 1) * P], ident[:])
                if t % TPB == TPB - 1:
                    mm.then_inc(s_yt, 1)


def project_phase(nc, dram, consts, x_tok, kr, v, q_scratch):
    nm = "pr_"
    ident = consts["ident"]
    with ExitStack() as ctx:
        def sb(name, shape, dt=F32):
            return ctx.enter_context(nc.sbuf_tensor(nm + name, shape, dt))

        def sem(name):
            return ctx.enter_context(nc.semaphore(nm + name))

        hT = sb("hT", [P, SEQ])
        h_tok = sb("h_tok", [P, NT, DIM])
        st, mv = sb("st", [P, NT, 6]), sb("mv", [P, NT, 2])
        var, rstd, small = sb("var", [P, NT]), sb("rstd", [P, NT]), sb("small", [P, 5, NT])
        wqk = sb("wqk", [P, 4 * DIM])
        wv = sb("wv", [P, DIM])
        rope = sb("rope", [P, 2, SEQ])
        sel_f = sb("sel_f", [P, 4, NG * P])
        sel = sb("sel", [P, 4, NG * P], F32R)
        ones = sb("ones_rows", [P, 1])
        ra, rbm, rr = (sb(n, [P, 2, BLK]) for n in ("rot_a", "rot_b", "rot"))
        rh, rl = sb("rot_hi", [P, 2, BLK], F32R), sb("rot_lo", [P, 2, BLK], F32R)
        qs = sb("qs", [P, 4, BLK], F32R)
        pj = ctx.enter_context(nc.psum_tensor(nm + "pj", [P, 4, BLK], F32))
        rp = ctx.enter_context(nc.psum_tensor(nm + "rp", [P, 4, BLK], F32))
        s_in, s_dve = sem("in"), sem("dve_chain")
        s_var, s_sqrt, s_h, s_tp, s_hT = sem("var"), sem("sqrt"), sem("h"), sem("tp"), sem("hT")
        s_selr, s_pj, s_pjr, s_rot, s_rh, s_rl = sem("sel"), sem("pj"), sem("pj_read"), sem("rot"), sem("rh"), sem("rl")
        s_rp, s_ev = sem("replicated"), sem("replicated_read")
        s_qst = [sem(f"q_stored{g}") for g in range(NG)]
        s_vp, s_ve, s_one = sem("v_done"), sem("v_read"), sem("v_ones")
        block = ctx.enter_context(nc.Block())

        @block.sync
        def _(sp):
            for dst, src in ((wqk[:], "wqk"), (wv[:], "wv"), (rope[:], "rope"), (sel_f[:], "sel"), (ones[:], "ones_rows")):
                sp.dma_start(dst, dram[src]).then_inc(s_in, 16)
            for b in range(NB):
                for gi in range(NG):
                    sp.wait_ge(s_ev, (2 * b) * NG + gi + 1)
                    sp.dma_start(q_scratch[b, gi], f32(qs[:, gi, :])).then_inc(s_qst[gi], 16)
            for gi in range(NG):
                sp.wait_ge(s_qst[gi], 16 * NB)

        @block.scalar
        def _(act):
            act.wait_ge(s_var, 1)
            nc.scalar.activation(small[:, 0, :], var[:], ACT.Sqrt).then_inc(s_sqrt, 1)
            act.wait_ge(s_in, 16 * 5)
            nc.scalar.copy(sel[:], sel_f[:]).then_inc(s_selr, 1)
            for b in range(NB):
                act.wait_ge(s_tp, b + 1)
                nc.scalar.copy(hT[:, b * BLK:(b + 1) * BLK], pj[:, b, :]).then_inc(s_hT, 1)
            for b in range(NB):
                for j in range(2):
                    J = 2 * b + j
                    act.wait_ge(s_rot, J + 1)
                    if J >= 2:
                        act.wait_ge(s_rp, (J - 1) * NG)
                    nc.scalar.copy(rh[:, j, :], rr[:, j, :]).then_inc(s_rh, 1)
                    for gi in range(NG):
                        act.wait_ge(s_rp, J * NG + gi + 1)
                        if j == 0:
                            if b:
                                act.wait_ge(s_qst[gi], 16 * b)
                            nc.scalar.copy(qs[:, gi, :], rp[:, gi, :]).then_inc(s_ev, 1)
                        else:
                            nc.scalar.activation(kr[:, gi, b * BLK:(b + 1) * BLK], rp[:, gi, :], ACT.Identity,
                                                 bias=ones[:, 0:1]).then_inc(s_ev, 1)

        @block.vector
        def _(dve):
            ch = Chain(dve, s_dve)
            layernorm_stats(nc, dve, ch, x_tok, st, mv, var, rstd, s_var, s_sqrt, small)
            for t in range(NT):
                nc.vector.tensor_scalar(h_tok[:, t, :], x_tok[:, t, :], mv[:, t, 0:1], small[:, 4, t:t + 1],
                                        ALU.subtract, ALU.mult).then_inc(s_h, 1)
            nc.vector.memset(v[:, :, :, DK:VW], 1.0).then_inc(s_one, 1)
            dve.wait_ge(s_in, 16 * 5)
            for b in range(NB):
                s = slice(b * BLK, (b + 1) * BLK)
                for j in range(2):
                    J = 2 * b + j
                    dve.wait_ge(s_pj, J + 1)
                    nc.vector.tensor_tensor(ra[:, j, :], pj[:, 2 * j, :], rope[:, 0, s], ALU.mult)
                    nc.vector.tensor_tensor(rbm[:, j, :], pj[:, 2 * j + 1, :], rope[:, 1, s], ALU.mult).then_inc(s_pjr, 1)
                    dve.wait_ge(s_pjr, J + 1)
                    if J >= 2:
                        dve.wait_ge(s_rl, J - 1)
                    nc.vector.tensor_tensor(rr[:, j, :], ra[:, j, :], rbm[:, j, :], ALU.add).then_inc(s_rot, 1)
                    dve.wait_ge(s_rh, J + 1)
                    nc.vector.tensor_tensor(rl[:, j, :], rr[:, j, :], f32(rh[:, j, :]), ALU.subtract).then_inc(s_rl, 1)
            for b in range(NB):
                dve.wait_ge(s_vp, b + 1)
                nc.vector.tensor_copy(v[:, b * TPB:(b + 1) * TPB, :, 0:DK].rearrange("p t h d -> p (t h) d"),
                                      pj[:, b, :].rearrange("p (n d) -> p n d", d=DK)).then_inc(s_ve, 1)

        @block.tensor
        def _(pe):
            for t in range(NT):
                pe.wait_ge(s_h, t + 1)
                mm = nc.tensor.transpose(pj[:, t // TPB, (t % TPB) * P:(t % TPB + 1) * P], h_tok[:, t, :], ident[:])
                if t % TPB == TPB - 1:
                    mm.then_inc(s_tp, 1)
            pe.wait_ge(s_in, 16 * 5)
            pe.wait_ge(s_selr, 1)
            pe.wait_ge(s_hT, NB)

            def project(J):
                b, j = J // 2, J % 2
                if J >= 2:
                    pe.wait_ge(s_pjr, J - 1)
                for m in range(2):
                    w = slice((2 * j + m) * DIM, (2 * j + m + 1) * DIM)
                    mm = nc.tensor.matmul(pj[:, 2 * j + m, :], wqk[:, w], hT[:, b * BLK:(b + 1) * BLK], start=True, stop=True)
                mm.then_inc(s_pj, 1)

            project(0)
            for J in range(2 * NB):
                if J + 1 < 2 * NB:
                    project(J + 1)
                j = J % 2
                pe.wait_ge(s_rl, J + 1)
                for gi in range(NG):
                    if J:
                        pe.wait_ge(s_ev, (J - 1) * NG + gi + 1)
                    w = slice(gi * P, (gi + 1) * P)
                    nc.tensor.matmul(rp[:, gi, :], sel[:, 2 * j, w], rh[:, j, :], start=True, stop=False)
                    mm = nc.tensor.matmul(rp[:, gi, :], sel[:, 2 * j + 1, w], rl[:, j, :], start=False, stop=True)
                    mm.then_inc(s_rp, 1)
            pe.wait_ge(s_pjr, 2 * NB)
            for t in range(NT):
                mm = nc.tensor.matmul(pj[:, t // TPB, (t % TPB) * P:(t % TPB + 1) * P], hT[:, t * P:(t + 1) * P], wv[:],
                                      start=True, stop=True)
                if t % TPB == TPB - 1:
                    mm.then_inc(s_vp, 1)


def attention_phase(nc, dram, consts, x_tok, kr, v, q_scratch):
    nm = "at_"
    ident, identr = consts["ident"], consts["identr"]
    STEPS = SEQ // P
    CHUNKS = SEQ // BLK
    MU = HG * TPB * CHUNKS
    PER = MU // STEPS
    LEAD = 3 * PER
    NGR = NB * NG
    RING = 3

    PROLOGUE = [("max", 0, u) for u in range(MU)] + [("max", 1, u) for u in range(PER)] + [("rows", 0, 0)]
    PROLOGUE += [("max", 1, u) for u in range(PER, LEAD)]
    WINDOW = [[("max", 1 + u // MU, u % MU) for u in range(LEAD + s * PER, LEAD + (s + 1) * PER)] for s in range(STEPS)]
    WINDOW[3].insert(0, ("acc", -1, 0))
    WINDOW[14].insert(0, ("rows", 1, 0))
    FLAT = [item for items in WINDOW for item in items]
    assert len(FLAT) % RING == 0


    def place(item):
        return FLAT.index(item)

    with ExitStack() as ctx:
        def sb(name, shape, dt=F32):
            return ctx.enter_context(nc.sbuf_tensor(nm + name, shape, dt))

        def sem(name):
            return ctx.enter_context(nc.semaphore(nm + name))

        def pb(name, shape):
            return ctx.enter_context(nc.psum_tensor(nm + name + "_ps", shape, F32))

        qm = [sb(f"qm{g}", [P, HG, BLK], F32R) for g in range(NG)]
        probs = sb("probs", [P, 4, 2 * BLK])
        mpart = sb("mpart", [P, 2, HG * TPB, CHUNKS])
        mx = sb("mx", [P, HG * TPB])
        mfull = sb("mfull", [P, TPB, P], F32R)
        mrows = sb("mrows", [P, BLK], F32R)
        acc_s = sb("acc_s", [P, BLK])
        rden = sb("rden", [P, TPB, HG])
        o_all = sb("o_all", [P, NT, DIM])
        oT = sb("oT", [P, 2, BLK])
        wo, wob = sb("wo", [P, DIM]), sb("wob", [P, DIM])
        st_ps = pb("st", [P, 2, 2 * BLK])
        ring = pb("ring", [P, RING, BLK])
        acc = pb("acc", [P, BLK])

        s_in, s_zero, s_init = sem("in"), sem("zeros"), sem("init")
        s_qm = [sem(f"queries_loaded{g}") for g in range(NG)]
        s_mrow = sem("max_rows_stored")
        s_st, s_exp, s_pv = sem("scores"), sem("exp"), sem("pv")
        s_mx, s_red, s_mm = sem("max_scores"), sem("max_reduced"), sem("max_chain")
        s_mt, s_mr = sem("max_transposed"), sem("max_rows")
        s_accs, s_at, s_rd, s_o = sem("acc_copied"), sem("acc_transposed"), sem("rden"), sem("o")
        s_ot, s_oc, s_pr, s_xb, s_xn = sem("oT"), sem("oT_copied"), sem("projected"), sem("x_bias"), sem("x_new")
        block = ctx.enter_context(nc.Block())

        def wait(eng, s, value):
            if not (isinstance(value, int) and value <= 0):
                eng.wait_ge(s, value)

        def groups(eng, group):
            group(0, 0, 0)
            with eng.Fori(0, NB - 1) as it:
                for k in range(1, NG + 1):
                    group(it * NG + k, k, it)
            for k in range(1, NG):
                group((NB - 1) * NG + k, k, NB - 1)

        def exists(G):
            return not isinstance(G, int) or G < NGR

        @block.sync
        def _(sp):
            for dst, src in ((wo[:], "wo"), (wob[:], "wob")):
                sp.dma_start(dst, dram[src]).then_inc(s_in, 16)

            def load_queries(k, it):
                g, b = k % NG, it + k // NG
                for h in range(HG):
                    rows = slice(QUAD * h, QUAD * (h + 1))
                    src = q_scratch[b, g, rows] if isinstance(b, int) else q_scratch[bass.ds(b, 1), g, rows].squeeze(0)
                    sp.dma_start(f32(qm[g][rows, h, :]), src).then_inc(s_qm[g], 16)

            def store_max_rows(k):
                for h in range(HG):
                    rows = slice(QUAD * h + ROW_M, QUAD * h + ROW_M + 2)
                    sp.dma_start(f32(qm[k % NG][rows, h, :]), f32(mrows[rows, :])).then_inc(s_mrow, 16)

            sp.wait_ge(s_zero, NG)
            for k in range(3):
                load_queries(k, 0)
            sp.wait_ge(s_mr, 1)
            store_max_rows(0)

            def group(G, k, it):
                if exists(G + 3):
                    wait(sp, s_st, G * 2 * STEPS)
                    load_queries(k + 3, it)
                if exists(G + 1):
                    sp.wait_ge(s_mr, G + 2)
                    store_max_rows(k + 1)

            groups(sp, group)

        @block.gpsimd
        def _(pool):
            for g in range(NG):
                nc.gpsimd.memset(f32(qm[g][:]), 0.0).then_inc(s_zero, 1)

        @block.scalar
        def _(act):
            def copy_max_rows(G, bank):
                wait(act, s_mt, G + 1)
                wait(act, s_mrow, G * 64)
                nc.scalar.copy(mrows[:], ring[:, bank, :]).then_inc(s_mr, 1)

            def copy_acc(G):
                wait(act, s_pv, G * STEPS + STEPS)
                nc.scalar.copy(acc_s[:], acc[:]).then_inc(s_accs, 1)

            copy_max_rows(0, (PROLOGUE.index(("rows", 0, 0)) - len(PROLOGUE)) % RING)

            def group(G, k, it):
                for s in range(STEPS):
                    T = G * STEPS + s
                    if s == 1 and k:
                        copy_acc(G - 1)
                    for pair in range(2):
                        if s == 14 and pair == 0 and exists(G + 1):
                            copy_max_rows(G + 1, place(("rows", 1, 0)) % RING)
                        act.wait_ge(s_st, T * 2 + pair + 1)
                        wait(act, s_pv, T - 1)
                        nc.scalar.activation(probs[:, 2 * (s % 2) + pair, :], st_ps[:, pair, :], ACT.Exp,
                                             scale=SCALE).then_inc(s_exp, 1)

            groups(act, group)
            copy_acc(NGR - 1)
            for b in range(NB):
                act.wait_ge(s_ot, b + 1)
                if b >= 2:
                    act.wait_ge(s_pr, b - 1)
                nc.scalar.copy(oT[:, b % 2, :], st_ps[:, 0, (b % 2) * BLK:(b % 2 + 1) * BLK]).then_inc(s_oc, 1)

        @block.vector
        def _(dve):
            nc.vector.memset(acc[:], 0.0).then_inc(s_init, 1)
            nc.vector.memset(f32(mfull[:]), 0.0).then_inc(s_init, 1)

            def reduce_max(G, k, u, bank):
                V = G * MU + u
                if u == 0:
                    wait(dve, s_mm, G * 3 - 3)
                dve.wait_ge(s_mx, V + 1)
                nc.vector.tensor_reduce(mpart[:, k % 2, u // CHUNKS, u % CHUNKS:u % CHUNKS + 1], ring[:, bank, :], AX_X, ALU.max).then_inc(s_red, 1)

            def negate_max(G, k):
                dve.wait_ge(s_red, G * MU + MU)
                nc.vector.tensor_reduce(mx[:], mpart[:, k % 2], AX_X, ALU.max).then_inc(s_mm, 1)
                dve.wait_ge(s_mm, G * 3 + 1)
                wait(dve, s_mt, G)
                mf = mfull[:].rearrange("p t (h r) -> p t h r", r=QUAD)
                mq = mx[:].rearrange("p (h t) -> p t h", t=TPB)
                if isinstance(G, int) and G == 0:
                    dve.wait_ge(s_init, 2)
                nc.vector.tensor_scalar(mf[:, :, :, ROW_M], mq, -1.0, None, ALU.mult).then_inc(s_mm, 1)
                dve.wait_ge(s_mm, G * 3 + 2)
                nc.vector.scalar_tensor_tensor(out=mf[:, :, :, ROW_M + 1], in0=mq, scalar=-1.0,
                                               in1=f32(mfull[:]).rearrange("p t (h r) -> p t h r", r=QUAD)[:, :, :, ROW_M],
                                               op0=ALU.mult, op1=ALU.subtract).then_inc(s_mm, 1)

            def normalize(G, k, it):
                b, g = it + k // NG, k % NG
                dve.wait_ge(s_at, G + 1)
                m4 = ring[:, place(("acc", -1, 0)) % RING, :].rearrange("p (t h r) -> p t h r", t=TPB, r=QUAD)
                nc.vector.reciprocal(rden[:], m4[:, :, :, DK]).then_inc(s_rd, 1)
                dve.wait_ge(s_rd, G + 1)
                tiles = slice(b * TPB, (b + 1) * TPB) if isinstance(b, int) else bass.ds(b * TPB, TPB)
                out = o_all[:, tiles, g * HG * DK:(g + 1) * HG * DK].rearrange("p t (h d) -> p t h d", d=DK)
                nc.vector.tensor_tensor(out, m4[:, :, :, 0:DK], rden[:].unsqueeze(3).to_broadcast([P, TPB, HG, DK]),
                                        ALU.mult).then_inc(s_o, 1)

            for n, (kind, G, u) in enumerate(PROLOGUE, -len(PROLOGUE)):
                if kind == "max":
                    reduce_max(G, G, u, n % RING)
                    if (G, u) == (0, MU - 1):
                        negate_max(0, 0)

            def group(G, k, it):
                for s in range(STEPS):
                    for item in WINDOW[s]:
                        kind, ahead, u = item
                        if kind == "acc" and k:
                            normalize(G - 1, k - 1, it)
                        elif kind == "max" and exists(G + ahead):
                            reduce_max(G + ahead, k + ahead, u, place(item) % RING)
                            if u == MU - 1:
                                negate_max(G + 1, k + 1)

            groups(dve, group)
            dve.wait_ge(s_in, 32)
            nc.vector.tensor_tensor(x_tok[:], x_tok[:], wob[:].unsqueeze(1).to_broadcast([P, NT, DIM]),
                                    ALU.add).then_inc(s_xb, 1)
            normalize(NGR - 1, NG - 1, NB - 1)
            dve.wait_ge(s_xb, 1)
            for b in range(NB):
                dve.wait_ge(s_pr, b + 1)
                xs = x_tok[:, b * TPB:(b + 1) * TPB, :]
                half = st_ps[:, 1, (b % 2) * BLK:(b % 2 + 1) * BLK].rearrange("p (t d) -> p t d", d=DIM)
                nc.vector.tensor_tensor(xs, xs, half, ALU.add).then_inc(s_xn, 1)

        @block.tensor
        def _(pe):
            def bank_free(G, n):
                while True:
                    n -= RING
                    if isinstance(G, int) and G * len(FLAT) + n < 0:
                        if n < -len(PROLOGUE):
                            return
                        kind, ahead, u = PROLOGUE[n]
                    else:
                        kind, ahead, u = FLAT[n % len(FLAT)]
                        ahead += n // len(FLAT)
                    if exists(G + ahead):
                        break
                if kind == "max":
                    pe.wait_ge(s_red, (G + ahead) * MU + u + 1)
                elif kind == "rows":
                    pe.wait_ge(s_mr, G + ahead + 1)
                else:
                    wait(pe, s_o, G + ahead + 1)

            def max_scores(G, k, it, u, bank):
                V, g = G * MU + u, k % NG
                h, t, c = u // (TPB * CHUNKS), u // CHUNKS % TPB, u % CHUNKS
                if u == 0:
                    pe.wait_ge(s_qm[g], 64 * (it + k // NG + 1))
                nc.tensor.matmul(ring[:, bank, :], qm[g][:, h, t * P:(t + 1) * P],
                                 kr[:, g, c * BLK:(c + 1) * BLK], start=True, stop=True).then_inc(s_mx, 1)

            def transpose_max(G, bank):
                pe.wait_ge(s_mm, G * 3 + 3)
                for t in range(TPB):
                    mm = nc.tensor.matmul(ring[:, bank, t * P:(t + 1) * P], mfull[:, t, :], identr[:], start=True, stop=True)
                mm.then_inc(s_mt, 1)

            def transpose_acc(G, bank):
                pe.wait_ge(s_accs, G + 1)
                for t in range(TPB):
                    mm = nc.tensor.transpose(ring[:, bank, t * P:(t + 1) * P], acc_s[:, t * P:(t + 1) * P], ident[:])
                mm.then_inc(s_at, 1)

            def scores(G, k, s, head):
                T, g, pair = G * STEPS + s, k % NG, head // 2
                if head % 2 == 0:
                    wait(pe, s_exp, T * 2 + pair - 1)
                mm = nc.tensor.matmul(st_ps[:, pair, head % 2 * BLK:(head % 2 + 1) * BLK], kr[:, g, s * P:(s + 1) * P],
                                      qm[g][:, head, :], start=True, stop=True)
                if head % 2:
                    mm.then_inc(s_st, 1)

            def values(G, k, s):
                g = k % NG
                pe.wait_ge(s_exp, G * 2 * STEPS + 2 * s + 2)
                if s == 0:
                    wait(pe, s_accs, G)
                for h in range(HG):
                    mm = nc.tensor.matmul(acc[QUAD * h:QUAD * h + VW, :], v[:, s, g * HG + h, :],
                                          probs[:, 2 * (s % 2) + h // 2, (h % 2) * BLK:(h % 2 + 1) * BLK],
                                          start=(s == 0), stop=(s == STEPS - 1), skip_group_check=True)
                mm.then_inc(s_pv, 1)

            for n, (kind, G, u) in enumerate(PROLOGUE, -len(PROLOGUE)):
                bank_free(0, n)
                if kind == "rows":
                    transpose_max(0, n % RING)
                else:
                    max_scores(G, G, 0, u, n % RING)
            pe.wait_ge(s_init, 2)

            def group(G, k, it):
                for s in range(STEPS):
                    if s == 0:
                        pe.wait_ge(s_mrow, G * 64 + 64)
                    units = []
                    for item in WINDOW[s]:
                        kind, ahead, u = item
                        n = place(item)
                        if not exists(G + ahead) or (kind == "acc" and k == 0):
                            continue
                        if kind == "max":
                            units.append((ahead, u, n))
                            continue
                        bank_free(G, n)
                        if kind == "acc":
                            transpose_acc(G - 1, n % RING)
                        else:
                            transpose_max(G + 1, n % RING)
                    for head in range(HG):
                        scores(G, k, s, head)
                        for ahead, u, n in units[head:head + 1]:
                            bank_free(G, n)
                            max_scores(G + ahead, k + ahead, it, u, n % RING)
                    if s:
                        values(G, k, s - 1)
                    elif k:
                        values(G - 1, k - 1, STEPS - 1)

            groups(pe, group)
            values(NGR - 1, NG - 1, STEPS - 1)
            bank_free(NGR, place(("acc", -1, 0)))
            transpose_acc(NGR - 1, place(("acc", -1, 0)) % RING)
            pe.wait_ge(s_o, NGR)
            pe.wait_ge(s_in, 32)
            for b in range(NB):
                if b >= 2:
                    pe.wait_ge(s_oc, b - 1)
                for t in range(TPB):
                    at = (b % 2) * BLK + t * P
                    mm = nc.tensor.transpose(st_ps[:, 0, at:at + P], o_all[:, b * TPB + t, :], ident[:])
                mm.then_inc(s_ot, 1)
                pe.wait_ge(s_oc, b + 1)
                if b >= 2:
                    pe.wait_ge(s_xn, b - 1)
                for t in range(TPB):
                    at = (b % 2) * BLK + t * P
                    mm = nc.tensor.matmul(st_ps[:, 1, at:at + P], oT[:, b % 2, t * P:(t + 1) * P], wo[:],
                                          start=True, stop=True)
                mm.then_inc(s_pr, 1)


def macaron_kernel(nc, dram):
    with ExitStack() as ctx:
        def sb(name, shape, dt=F32):
            return ctx.enter_context(nc.sbuf_tensor(name, shape, dt))

        x_tok = sb("x_tok", [P, NT, DIM])
        w1h, w1l = sb("w1h", [P, E * INNER], F32R), sb("w1l", [P, E * INNER], F32R)
        w2h, w2l = sb("w2h", [P, E * INNER], F32R), sb("w2l", [P, E * INNER], F32R)
        b2h, b2l = sb("b2h", [P, DIM], F32R), sb("b2l", [P, DIM], F32R)
        rwh, rwl = sb("rwh", [P, E], F32R), sb("rwl", [P, E], F32R)
        consts = {
            "ident": sb("ident", [P, P]), "identr": sb("identr", [P, P], F32R),
            "onehot": sb("onehot", [P, E * P], F32R), "b1": sb("b1", [P, E * HALVES]), "rb": sb("rb", [P, E]),
        }
        weights = (w1h, w1l, w2h, w2l, b2h, b2l, rwh, rwl)
        q_scratch = nc.dram_tensor("q_scratch", [NB, NG, P, BLK], F32, kind="Internal").ap()
        ffn_phase(nc, "f1_", dram, consts, x_tok, weights, first=True)
        with ExitStack() as kv:
            kr = kv.enter_context(nc.sbuf_tensor("kr", [P, NG, SEQ], F32R))
            v = kv.enter_context(nc.sbuf_tensor("v", [P, NT, HEADS, VW], F32))
            project_phase(nc, dram, consts, x_tok, kr, v, q_scratch)
            attention_phase(nc, dram, consts, x_tok, kr, v, q_scratch)
        ffn_phase(nc, "f2_", dram, consts, x_tok, weights, first=False)


def shape_constants(np):
    even, odd = np.arange(0, DIM, 2), np.arange(1, DIM, 2)
    pos = np.arange(SEQ, dtype=np.float32)
    freqs = np.exp(np.arange(0, DIM, 2, dtype=np.float32) * np.float32(-np.log(10000.0) / DIM)).astype(np.float32)
    ang = (freqs[:, None] * pos[None, :]).astype(np.float32)
    cos, sin = np.cos(ang), np.sin(ang)
    rope = np.stack([np.concatenate([cos, cos]), np.concatenate([-sin, sin])], axis=1).astype(np.float32)
    onehot = np.zeros((P, E, P), np.float32)
    for e in range(E):
        onehot[e, e] = onehot[E + e, e] = 1.0
    sel = np.zeros((P, 4, NG, HG, QUAD), np.float32)
    rows = (((0, 2)), (1,), (0, 1), (2,))
    for f, thirds in enumerate(rows):
        for third in thirds:
            for g in range(NG):
                for h in range(HG):
                    for d in range(DK):
                        sel[(g * HG + h) * DK + d, f, g, h, third * DK + d] = 1.0
    ones_rows = np.zeros((HG, QUAD), np.float32)
    ones_rows[:, ROW_M:ROW_M + 2] = 1.0
    return {"rope": rope, "onehot": onehot.reshape(P, E * P), "sel": sel.reshape(P, 4, NG * P),
            "ones_rows": ones_rows.reshape(P, 1), "ident": np.eye(P, dtype=np.float32),
            "perm_a": np.concatenate([even, odd]), "perm_b": np.concatenate([odd, even])}


def kernel(L0_attn_x, L0_attn_wq, L0_attn_wk, L0_attn_wv, L0_attn_wo_w, L0_attn_wo_b, L0_ffn_router_w,
           L0_ffn_router_b, L0_ffn_w1, L0_ffn_b1, L0_ffn_w2, L0_ffn_b2):
    import numpy as np
    import concourse.bacc as bacc
    from concourse.bass_utils import run_bass_kernel_spmd

    c = shape_constants(np)
    pa, pb = c.pop("perm_a"), c.pop("perm_b")
    wq, wk = np.asarray(L0_attn_wq), np.asarray(L0_attn_wk)
    arrays = {
        "x": np.asarray(L0_attn_x).reshape(SEQ, DIM),
        "wqk": np.concatenate([wq[pa].T, wq[pb].T, wk[pa].T, wk[pb].T], axis=1),
        "wv": np.asarray(L0_attn_wv).T, "wo": np.asarray(L0_attn_wo_w).T,
        "wob": np.broadcast_to(np.asarray(L0_attn_wo_b), (P, DIM)),
        "rw": np.asarray(L0_ffn_router_w), "rb": np.broadcast_to(np.asarray(L0_ffn_router_b), (P, E)),
        "w1": np.asarray(L0_ffn_w1), "w2": np.asarray(L0_ffn_w2),
        "b1": np.asarray(L0_ffn_b1).reshape(E, HALVES, P).transpose(2, 0, 1).reshape(P, E * HALVES),
        "b2": np.concatenate([np.asarray(L0_ffn_b2)] * 2 + [np.zeros((P - 2 * E, DIM), np.float32)], axis=0),
        **c,
    }
    arrays = {n: np.ascontiguousarray(a) for n, a in arrays.items()}
    nc = bacc.Bacc("TRN2", target_bir_lowering=False, num_devices=1)
    dram = {n: nc.dram_tensor("in_" + n, a.shape, F32, kind="ExternalInput").ap() for n, a in arrays.items()}
    dram["out"] = nc.dram_tensor("out", (SEQ, DIM), F32, kind="ExternalOutput").ap()
    macaron_kernel(nc, dram)
    r = run_bass_kernel_spmd(nc, [{"in_" + n: a for n, a in arrays.items()}], core_ids=[0])
    return r.results[0]["out"].reshape(1, SEQ, DIM)
```

```python
from contextlib import ExitStack

import concourse.bass as bass
from concourse import mybir

F32 = mybir.dt.float32
F32R = mybir.dt.float32r
ALU = mybir.AluOpType
ACT = mybir.ActivationFunctionType
AX_X = mybir.AxisListType.X

P = 128
SEQ = 2048
DIM = 128
NT = SEQ // P
BLK = 512
NB = SEQ // BLK
TPB = BLK // P
E = 16
TOPK = 4
INNER = 256
HALVES = INNER // P
UNITS = E * HALVES
TURN = 10
HEADS = 16
DK = DIM // HEADS
HG = 4
NG = HEADS // HG
QUAD = 32
ROW_M = 3 * DK
VW = DK + 1
EPS = 1e-5
SCALE = DK ** -0.5


def f32(ap):
    return ap.bitcast(F32)


class Chain:

    def __init__(self, eng, sem):
        self.eng, self.sem, self.n = eng, sem, 0

    def link(self, ins):
        ins.then_inc(self.sem, 1)
        self.n += 1
        self.eng.wait_ge(self.sem, self.n)


def blocks_loop(eng, step):
    for u in range(TURN):
        step(0, u)
    with eng.Fori(0, NB - 1) as it:
        for u in range(TURN, UNITS):
            step(it, u)
        for u in range(TURN):
            step(it + 1, u)
    for u in range(TURN, UNITS):
        step(NB - 1, u)


def tile(tok, t):
    return tok[:, t, :] if isinstance(t, int) else tok[:, bass.ds(t, 1), :].squeeze(1)


def block_tiles(tok, b):
    return tok[:, b * TPB:(b + 1) * TPB, :] if isinstance(b, int) else tok[:, bass.ds(b * TPB, TPB), :]


def block_stats(nc, chain, x_tok, st, mv, b):
    for t in range(b * TPB, (b + 1) * TPB):
        last = nc.vector.bn_stats(st[:, t, :], x_tok[:, t, :])
    chain.link(last)
    for t in range(b * TPB, (b + 1) * TPB):
        last = nc.vector.bn_aggr(mv[:, t, :], st[:, t, :])
    chain.link(last)


def inverse_deviation(nc, dve, chain, mv, var, small, sem_var, sem_sqrt):
    nc.vector.tensor_scalar(var[:], mv[:, :, 1], EPS, None, ALU.add).then_inc(sem_var, 1)
    dve.wait_ge(sem_sqrt, 1)
    chain.link(nc.vector.reciprocal(small[:, 1, :], small[:, 0, :]))
    chain.link(nc.vector.tensor_tensor(small[:, 2, :], small[:, 1, :], small[:, 1, :], ALU.mult))
    chain.link(nc.vector.tensor_tensor(small[:, 3, :], small[:, 2, :], var[:], ALU.mult))
    chain.link(nc.vector.tensor_scalar(small[:, 2, :], small[:, 3, :], -0.5, 1.5, ALU.mult, ALU.add))
    chain.link(nc.vector.tensor_tensor(small[:, 4, :], small[:, 2, :], small[:, 1, :], ALU.mult))


def normalize_block(nc, x_tok, mv, small, h_tok, b, sem_h):
    for t in range(b * TPB, (b + 1) * TPB):
        last = nc.vector.tensor_scalar(h_tok[:, t, :], x_tok[:, t, :], mv[:, t, 0:1], small[:, 4, t:t + 1],
                                       ALU.subtract, ALU.mult)
    last.then_inc(sem_h, 1)


def transpose_block(nc, bank, tok, b, ident, sem):
    for t in range(TPB):
        last = nc.tensor.transpose(bank[:, t * P:(t + 1) * P], tok[:, b * TPB + t, :], ident[:])
    last.then_inc(sem, 1)


def ffn_phase(nc, nm, dram, consts, x_tok, st, mv, weights, first, ahead=None):
    w1h, w1l, w2h, w2l, b2h, b2l, rw2 = weights
    ident, identr, onehot, b1, rb = (consts[n] for n in ("ident", "identr", "onehot", "b1", "rb"))
    with ExitStack() as ctx:
        def sb(name, shape, dt=F32):
            return ctx.enter_context(nc.sbuf_tensor(nm + name, shape, dt))

        def pb(name, shape):
            return ctx.enter_context(nc.psum_tensor(nm + name + "_ps", shape, F32))

        def sem(name):
            return ctx.enter_context(nc.semaphore(nm + name))

        hh = sb("hh", [P, SEQ], F32R)
        hl = sb("hl", [P, SEQ], F32R)
        var, small = sb("var", [P, NT]), sb("small", [P, 5, NT])
        lg, ex, gt, eq, cs = (sb(n, [P, NT, E]) for n in ("lg", "ex", "gt", "eq", "cs"))
        first_e = sb("first_e", [P, NT, E])
        top8 = sb("top8", [P, NT, 8])
        tot, rtot = sb("tot", [P, NT]), sb("rtot", [P, NT])
        ct = sb("ct", [P, NT, E])
        c2 = sb("c2", [P, NT, P], F32R)
        c2T = sb("c2T", [P, SEQ], F32R)
        g = sb("g", [P, 2, BLK])
        gc = sb("gc", [P, 4, BLK])
        gh, gl = sb("gh", [P, 4, BLK], F32R), sb("gl", [P, 4, BLK], F32R)
        h_tok = gc[:].rearrange("p a (t d) -> p (a t) d", d=DIM)
        yl = sb("y_or_logits", [P, SEQ])
        mv_b = sb("mv_b", [P, TPB, 2])
        warm = sb("warm", [P, 1])
        lT = yl[0:2 * E, :]
        yT = yl[:, 0:BLK]
        mid = pb("mid", [P, 4, BLK])
        cb = pb("cb", [P, 2, BLK])
        acc, aux = pb("acc", [P, BLK]), pb("aux", [P, BLK])
        c2_banks = (cb[:, 0, :], cb[:, 1, :], acc[:], aux[:])

        CH = 1024
        NCH = E * INNER // CH
        if first:
            w1f, w2f = sb("w1f", [P, E * INNER]), sb("w2f", [P, E * INNER])
            b2f, rwf = sb("b2f", [P, DIM]), sb("rwf", [P, E])
            s_x = [sem(f"x{b}") for b in range(NB)]
            s_small = sem("small_in")
            s_w = [[sem(f"w{m + 1}_{c}") for c in range(NCH)] for m in range(2)]
            s_hi, s_small_lo = sem("weights_hi"), sem("small_lo")
            s_wlo, s_rw, s_ahead = sem("weights_lo"), sem("router_zeros"), sem("loaded_ahead")
            wqk, wv, sel = ahead
            onehot_in = yl[0:2 * E, :]
            sel_in = w1f[:, 0:4 * NG * P].rearrange("p (f c) -> p f c", f=4)
            s_tables, s_onehot, s_hi_last = sem("tables"), sem("onehot_loaded"), sem("weights_hi_last_chunk")
        s_out = sem("out")
        s_dve, s_act = sem("dve_chain"), sem("act_chain")
        s_var, s_sqrt, s_h = sem("var"), sem("sqrt"), sem("h_tok")
        s_tp, s_hh, s_hl = sem("h_transposed"), sem("hh"), sem("hl")
        s_lg, s_lm, s_ex, s_c2 = sem("logits"), sem("logits_less_max"), sem("exp"), sem("c2")
        s_ctp, s_c2T = sem("c2_transposed"), sem("c2T")
        s_mid, s_gelu, s_cb, s_gc = sem("mid"), sem("gelu"), sem("cb"), sem("gc")
        s_ghi, s_glo, s_down, s_acc = sem("gh"), sem("gl"), sem("down"), sem("acc_copied")
        s_yt, s_xn = sem("y_transposed"), sem("x_new")
        s_lt, s_ltc, s_init = sem("logits_T"), sem("logits_T_copied"), sem("init")
        s_stats, s_aggr, s_mv = sem("stats"), sem("aggregated"), sem("mean_var")
        SLOTS = 4
        block = ctx.enter_context(nc.Block())

        @block.sync
        def _(sp):
            if first:
                xv = dram["x"].rearrange("(t p) d -> p t d", p=P)
                for b in range(NB):
                    sp.dma_start(x_tok[:, b * TPB:(b + 1) * TPB, :], xv[:, b * TPB:(b + 1) * TPB, :]).then_inc(s_x[b], 16)
                epc = CH // INNER
                for c in range(NCH):
                    sp.dma_start(w1f[:, c * CH:(c + 1) * CH].rearrange("p (e i) -> p e i", i=INNER),
                                 dram["w1"][c * epc:(c + 1) * epc].rearrange("e p i -> p e i")).then_inc(s_w[0][c], 16)
                    sp.dma_start(w2f[:, c * CH:(c + 1) * CH].rearrange("p (e t h) -> p e t h", t=HALVES, h=DIM),
                                 dram["w2"][c * epc:(c + 1) * epc].rearrange("e (t p) h -> p e t h", p=P)).then_inc(s_w[1][c], 16)
                for dst, src in ((wqk[:], "wqk"), (wv[:], "wv"), (sel_in, "sel")):
                    sp.wait_ge(s_wlo, 2 * NCH)
                    sp.dma_start(dst, dram[src]).then_inc(s_ahead, 16)
                sp.wait_ge(s_ahead, 16 * 3)
            else:
                ov = dram["out"].rearrange("(t p) d -> p t d", p=P)
                for b in range(NB):
                    sp.wait_ge(s_xn, b + 1)
                    sp.dma_start(ov[:, b * TPB:(b + 1) * TPB, :], x_tok[:, b * TPB:(b + 1) * TPB, :]).then_inc(s_out, 16)
                sp.wait_ge(s_out, 16 * NB)

        @block.gpsimd
        def _(pool):
            if first:
                nc.gpsimd.memset(f32(onehot[:]), 0.0).then_inc(s_onehot, 1)
                pool.wait_ge(s_small, 16 * 5)
                pool.wait_ge(s_onehot, 16 + 1)
                nc.gpsimd.tensor_copy(onehot[0:2 * E, :], onehot_in).then_inc(s_tables, 1)
                nc.gpsimd.tensor_copy(identr[:], ident[:]).then_inc(s_tables, 1)
            nc.gpsimd.memset(f32(c2[:]), 0.0).then_inc(s_init, 1)
            nc.gpsimd.memset(first_e[:], 1.0).then_inc(s_init, 1)
            if first:
                for c in range(NCH):
                    for m, (dst, src, hi) in enumerate(((w1l, w1f, w1h), (w2l, w2f, w2h))):
                        s = slice(c * CH, (c + 1) * CH)
                        if c == NCH - 1:
                            pool.wait_ge(s_w[m][c], 16)
                            nc.gpsimd.tensor_copy(hi[:, s], src[:, s]).then_inc(s_hi_last, 1)
                            pool.wait_ge(s_hi_last, m + 1)
                        else:
                            pool.wait_ge(s_hi, 2 + 2 * c + m + 1)
                        nc.gpsimd.tensor_tensor(dst[:, s], src[:, s], f32(hi[:, s]), ALU.subtract).then_inc(s_wlo, 1)
                pool.wait_ge(s_ahead, 16 * 3)
                nc.gpsimd.tensor_copy(sel[:], sel_in).then_inc(s_tables, 1)

        @block.scalar
        def _(act):
            if first:
                for dst, src in ((ident[:], "ident"), (b1[:], "b1"), (rb[:], "rb"), (b2f[:], "b2"), (rwf[:], "rw")):
                    act.dma_start(dst, dram[src]).then_inc(s_small, 16)
                act.dma_start(onehot_in, dram["onehot"]).then_inc(s_onehot, 16)
                act.wait_ge(s_small, 16 * 5)
                act.wait_ge(s_rw, 1)
                for dst, src in ((rw2[:, 0:E], rwf[:]), (b2h[:], b2f[:])):
                    nc.scalar.copy(dst, src).then_inc(s_hi, 1)
            act.wait_ge(s_var, 1)
            nc.scalar.activation(small[:, 0, :], var[:], ACT.Sqrt).then_inc(s_sqrt, 1)
            if first:
                def split_high(c):
                    for m, (dst, src) in enumerate(((w1h, w1f), (w2h, w2f))):
                        act.wait_ge(s_w[m][c], 16)
                        nc.scalar.copy(dst[:, c * CH:(c + 1) * CH], src[:, c * CH:(c + 1) * CH]).then_inc(s_hi, 1)

                split_high(0)

            def copy_logits(b):
                if first and b == 0:
                    act.wait_ge(s_tables, 1)
                act.wait_ge(s_lt, b + 1)
                nc.scalar.activation(lT[:, b * BLK:(b + 1) * BLK], cb[0:2 * E, b % 2, :],
                                     ACT.Identity, bias=rb[0:2 * E, 0:1]).then_inc(s_ltc, 1)

            for b in range(NB):
                act.wait_ge(s_tp, b + 1)
                nc.scalar.copy(hh[:, b * BLK:(b + 1) * BLK], mid[:, b, :]).then_inc(s_hh, 1)
                if b:
                    copy_logits(b - 1)
            copy_logits(NB - 1)
            if first:
                split_high(1)
            act.wait_ge(s_lm, 1)
            nc.scalar.activation(ex[:], lg[:], ACT.Exp).then_inc(s_ex, 1)
            if first:
                split_high(2)

            act.sem_inc(s_gelu, SLOTS)
            act.sem_inc(s_acc, 1)

            def gelu(b, u):
                act.wait_ge(s_mid, b * UNITS + u + 1)
                nc.scalar.activation(g[:, u % 2, :], mid[:, u % 4, :], ACT.Gelu,
                                     bias=b1[:, u % UNITS:u % UNITS + 1]).then_inc(s_gelu, 1)

            def copy_c2T(b):
                act.wait_ge(s_ctp, b + 1)
                nc.scalar.copy(c2T[:, b * BLK:(b + 1) * BLK], c2_banks[b]).then_inc(s_c2T, 1)

            def step(b, u):
                if not (isinstance(b, int) and (b, u) in ((0, 0), (NB - 1, UNITS - 1))):
                    gelu(b, u + 1)
                act.wait_ge(s_gc, b * UNITS + u + 1)
                act.wait_ge(s_down, b * UNITS + u + 1)
                nc.scalar.copy(gh[:, u % 4, :], gc[:, u % 4, :]).then_inc(s_ghi, 1)
                if isinstance(b, int) and b == 0:
                    if u + 2 < NB:
                        copy_c2T(u + 2)
                elif u == 1:
                    copy_acc(b - 1)

            def copy_acc(b):
                act.wait_ge(s_down, SLOTS + (b + 1) * UNITS)
                nc.scalar.copy(yT, acc[:]).then_inc(s_acc, 1)

            gelu(0, 0)
            gelu(0, 1)
            copy_c2T(0)
            copy_c2T(1)
            blocks_loop(act, step)
            if first:
                nc.scalar.activation(warm[:], ident[:, 0:1], ACT.Sqrt)
            copy_acc(NB - 1)

        @block.vector
        def _(dve):
            ch = Chain(dve, s_dve)
            if first:
                nc.vector.memset(f32(rw2[:]), 0.0).then_inc(s_rw, 1)
                for b in range(NB):
                    dve.wait_ge(s_x[b], 16)
                    block_stats(nc, ch, x_tok, st, mv, b)
            if first:
                dve.wait_ge(s_hi, 2)
                nc.vector.tensor_tensor(rw2[:, E:2 * E], rwf[:], f32(rw2[:, 0:E]), ALU.subtract).then_inc(s_small_lo, 1)
                nc.vector.tensor_tensor(b2l[:], b2f[:], f32(b2h[:]), ALU.subtract).then_inc(s_small_lo, 1)
            inverse_deviation(nc, dve, ch, mv, var, small, s_var, s_sqrt)
            normalize_block(nc, x_tok, mv, small, h_tok, 0, s_h)
            for b in range(NB):
                if b + 1 < NB:
                    normalize_block(nc, x_tok, mv, small, h_tok, b + 1, s_h)
                dve.wait_ge(s_hh, b + 1)
                s = slice(b * BLK, (b + 1) * BLK)
                nc.vector.tensor_tensor(hl[:, s], mid[:, b, :], f32(hh[:, s]), ALU.subtract).then_inc(s_hl, 1)
            dve.wait_ge(s_init, 2)
            ch.link(nc.vector.memset(first_e[:, :, 0:1], 0.0))
            dve.wait_ge(s_lg, 1)
            ch.link(nc.vector.tensor_reduce(lg[:], acc[:].rearrange("p (t s e) -> p t e s", s=2, e=E), AX_X, ALU.add))
            for t in range(NT):
                last = nc.vector.max(top8[:, t, :], lg[:, t, :])
            ch.link(last)
            thr = top8[:, :, TOPK - 1:TOPK].to_broadcast([P, NT, E])
            nc.vector.tensor_tensor(gt[:], lg[:], thr, ALU.is_gt)
            ch.link(nc.vector.tensor_tensor(eq[:], lg[:], thr, ALU.is_equal))
            nc.vector.tensor_tensor(lg[:], lg[:], top8[:, :, 0:1].to_broadcast([P, NT, E]),
                                    ALU.subtract).then_inc(s_lm, 1)
            flat = "p t e -> p (t e)"
            nc.vector.tensor_tensor_scan(cs[:].rearrange(flat), first_e[:].rearrange(flat), eq[:].rearrange(flat), 0.0,
                                         ALU.mult, ALU.add)
            ch.link(nc.vector.tensor_reduce(tot[:], gt[:], AX_X, ALU.add))
            ch.link(nc.vector.scalar_tensor_tensor(out=ct[:], in0=cs[:], scalar=-float(TOPK),
                                                   in1=tot[:].unsqueeze(2).to_broadcast([P, NT, E]),
                                                   op0=ALU.add, op1=ALU.add))
            ch.link(nc.vector.scalar_tensor_tensor(out=eq[:], in0=ct[:], scalar=0.0, in1=eq[:], op0=ALU.is_le, op1=ALU.mult))
            ch.link(nc.vector.tensor_tensor(gt[:], gt[:], eq[:], ALU.add))
            dve.wait_ge(s_ex, 1)
            ch.link(nc.vector.tensor_tensor(ex[:], ex[:], gt[:], ALU.mult))
            ch.link(nc.vector.tensor_reduce(tot[:], ex[:], AX_X, ALU.add))
            ch.link(nc.vector.reciprocal(rtot[:], tot[:]))
            ch.link(nc.vector.scalar_tensor_tensor(out=ct[:], in0=ex[:], scalar=0.5,
                                                   in1=rtot[:].unsqueeze(2).to_broadcast([P, NT, E]),
                                                   op0=ALU.mult, op1=ALU.mult))
            ch.link(nc.vector.tensor_copy(c2[:, :, 0:E], ct[:]))
            nc.vector.tensor_tensor(c2[:, :, E:2 * E], ct[:], f32(c2[:])[:, :, 0:E], ALU.subtract).then_inc(s_c2, 1)

            dve.sem_inc(s_glo, SLOTS)

            def gate(b, u):
                U = b * UNITS + u
                dve.wait_ge(s_gelu, U + 1 + SLOTS)
                dve.wait_ge(s_cb, b * E + u // HALVES + 1)
                dve.wait_ge(s_glo, U + 1)
                nc.vector.tensor_tensor(gc[:, u % 4, :], g[:, u % 2, :], cb[:, u // HALVES % 2, :],
                                        ALU.mult).then_inc(s_gc, 1)

            def step(b, u):
                if not (isinstance(b, int) and (b, u) == (NB - 1, UNITS - 1)):
                    gate(b, u + 1)
                U = b * UNITS + u
                finishing = not (isinstance(b, int) and b == 0) and u in FINISH
                if finishing:
                    finish_wait(b - 1, FINISH.index(u))
                dve.wait_ge(s_ghi, U + 1)
                dve.wait_ge(s_down, U + 1)
                nc.vector.tensor_tensor(gl[:, u % 4, :], gc[:, u % 4, :], f32(gh[:, u % 4, :]),
                                        ALU.subtract).then_inc(s_glo, 1)
                if finishing:
                    finish(b - 1, FINISH.index(u))

            FINISH = (5, 6, 7, 9)

            def finish_wait(b, part):
                if part == 0 or first:
                    dve.wait_ge((s_yt, s_xn, s_stats, s_aggr)[part], b + 1)

            def finish(b, part):
                if part == 0:
                    nc.vector.tensor_tensor(block_tiles(x_tok, b), block_tiles(x_tok, b), aux[:].rearrange("p (t d) -> p t d", d=DIM),
                                            ALU.add).then_inc(s_xn, 1)
                elif first:
                    if part == 3:
                        nc.vector.tensor_copy(block_tiles(mv, b), mv_b[:]).then_inc(s_mv, 1)
                        return
                    for t in range(TPB):
                        if part == 1:
                            last = nc.vector.bn_stats(st[:, t, :], tile(x_tok, b * TPB + t))
                        else:
                            last = nc.vector.bn_aggr(mv_b[:, t, :], st[:, t, :])
                    last.then_inc((s_stats, s_aggr)[part - 1], 1)

            gate(0, 0)
            blocks_loop(dve, step)
            for part in range(len(FINISH)):
                finish_wait(NB - 1, part)
                finish(NB - 1, part)

        @block.tensor
        def _(pe):
            if first:
                pe.wait_ge(s_small, 16 * 5)

            def transpose_h(b):
                pe.wait_ge(s_h, b + 1)
                transpose_block(nc, mid[:, b, :], h_tok, b, ident, s_tp)

            def logits(b):
                pe.wait_ge(s_hl, b + 1)
                if b >= 2:
                    pe.wait_ge(s_ltc, b - 1)
                s = slice(b * BLK, (b + 1) * BLK)
                nc.tensor.matmul(cb[:, b % 2, :], rw2[:], hh[:, s], start=True, stop=False)
                nc.tensor.matmul(cb[:, b % 2, :], rw2[:], hl[:, s], start=False, stop=True).then_inc(s_lt, 1)

            def logits_to_tokens(b):
                pe.wait_ge(s_ltc, b + 1)
                for t in range(b * TPB, (b + 1) * TPB):
                    last = nc.tensor.transpose(acc[:, t * 2 * E:(t + 1) * 2 * E], lT[:, t * P:(t + 1) * P],
                                               ident[0:2 * E, 0:2 * E])
                if b == NB - 1:
                    last.then_inc(s_lg, 1)

            transpose_h(0)
            transpose_h(1)
            if first:
                pe.wait_ge(s_small_lo, 1)
            for b in range(NB):
                logits(b)
                if b + 2 < NB:
                    transpose_h(b + 2)
                if b:
                    logits_to_tokens(b - 1)
            logits_to_tokens(NB - 1)

            def mids(b, u):
                e, half = u % UNITS // HALVES, u % HALVES
                U = b * UNITS + u
                if not (isinstance(U, int) and U < 4):
                    pe.wait_ge(s_gelu, U + 1)
                w = slice(e * INNER + half * P, e * INNER + (half + 1) * P)
                if first and u < UNITS and w.start % CH == 0:
                    pe.wait_ge(s_wlo, 2 * (w.start // CH) + 1)
                ts = bass.ts(b + u // UNITS, BLK)
                for n, (wp, hp) in enumerate(((w1h, hh), (w1h, hl), (w1l, hh))):
                    mm = nc.tensor.matmul(mid[:, u % 4, :], wp[:, w], hp[:, ts], start=(n == 0), stop=(n == 2))
                mm.then_inc(s_mid, 1)

            def spread(b, e):
                G = b * E + e
                if not (isinstance(G, int) and G < 2):
                    pe.wait_ge(s_gc, 2 * G - 2)
                nc.tensor.matmul(cb[:, e % 2, :], onehot[:, e % E * P:(e % E + 1) * P], c2T[:, bass.ts(b + e // E, BLK)],
                                 start=True, stop=True).then_inc(s_cb, 1)

            for u in range(3):
                mids(0, u)
            pe.wait_ge(s_c2, 1)
            if first:
                pe.wait_ge(s_tables, 2)
            for b in range(NB):
                for t in range(TPB):
                    mm = nc.tensor.matmul(c2_banks[b][:, t * P:(t + 1) * P], c2[:, b * TPB + t, :], identr[:],
                                          start=True, stop=True)
                mm.then_inc(s_ctp, 1)
                if b in (1, 2):
                    pe.wait_ge(s_c2T, b)
                    spread(0, b - 1)
            if first:
                pe.wait_ge(s_small_lo, 2)
            pe.sem_inc(s_down, SLOTS)
            LEAD = 3

            def step(b, u):
                last = isinstance(b, int) and b == NB - 1
                if not (last and u + LEAD >= UNITS):
                    mids(b, u + LEAD)
                    if (u + LEAD) % HALVES == 0:
                        spread(b, (u + LEAD) // HALVES)
                e, half = u // HALVES, u % HALVES
                if u == 0:
                    if isinstance(b, int) and b == 0:
                        pe.wait_ge(s_c2T, NB - 1)
                    pe.wait_ge(s_acc, b + 1)
                    for n, b2 in enumerate((b2h, b2l)):
                        nc.tensor.matmul(acc[:], b2[:], c2T[:, bass.ts(b, BLK)], start=(n == 0), stop=False)
                pe.wait_ge(s_glo, b * UNITS + u + 1 + SLOTS)
                w = slice((e * HALVES + half) * DIM, (e * HALVES + half + 1) * DIM)
                if first and w.start % CH == 0:
                    pe.wait_ge(s_wlo, 2 * (w.start // CH) + 2)
                for n, (wp, gp) in enumerate(((w2h, gh), (w2h, gl), (w2l, gh))):
                    mm = nc.tensor.matmul(acc[:], wp[:, w], gp[:, u % 4, :], start=False,
                                          stop=(u == UNITS - 1 and n == 2))
                mm.then_inc(s_down, 1)
                if u == 3:
                    if isinstance(b, int) and b == 0:
                        pe.wait_ge(s_c2T, NB)
                    else:
                        transpose_y(b - 1)

            def transpose_y(b):
                pe.wait_ge(s_acc, b + 2)
                for t in range(TPB):
                    mm = nc.tensor.transpose(aux[:, t * P:(t + 1) * P], yT[:, t * P:(t + 1) * P], ident[:])
                mm.then_inc(s_yt, 1)

            blocks_loop(pe, step)
            transpose_y(NB - 1)


def load_queries(sp, qm, s_qm, q_scratch, b, g):
    for h in range(HG):
        rows = slice(QUAD * h, QUAD * (h + 1))
        src = q_scratch[b, g, rows] if isinstance(b, int) else q_scratch[bass.ds(b, 1), g, rows].squeeze(0)
        sp.dma_start(f32(qm[g][rows, h, :]), src).then_inc(s_qm[g], 16)


def project_phase(nc, dram, consts, x_tok, mv, kr, hT, wqk, sel, qm, s_qm, q_scratch):
    nm = "pr_"
    ident = consts["ident"]
    with ExitStack() as ctx:
        def sb(name, shape, dt=F32):
            return ctx.enter_context(nc.sbuf_tensor(nm + name, shape, dt))

        def sem(name):
            return ctx.enter_context(nc.semaphore(nm + name))

        work = sb("work", [P, 4, BLK])
        h_tok = work[:].rearrange("p a (t d) -> p (a t) d", d=DIM)
        ra, rbm = work[:, 0:2, :], work[:, 2:4, :]
        var, small = sb("var", [P, NT]), sb("small", [P, 5, NT])
        RB = 3
        rope = sb("rope", [P, RB, 2, BLK])
        ones = sb("ones_rows", [P, 1])
        rr = sb("rot", [P, 2, BLK])
        rh, rl = sb("rot_hi", [P, 2, BLK], F32R), sb("rot_lo", [P, 2, BLK], F32R)
        qs = sb("qs", [P, 4, BLK], F32R)
        pj = ctx.enter_context(nc.psum_tensor(nm + "pj", [P, 4, BLK], F32))
        rp = ctx.enter_context(nc.psum_tensor(nm + "rp", [P, 4, BLK], F32))
        s_ones, s_zero, s_dve = sem("ones_loaded"), sem("zeros"), sem("dve_chain")
        s_rope = [sem(f"rope{b}") for b in range(NB)]
        s_var, s_sqrt, s_h, s_tp, s_hT = sem("var"), sem("sqrt"), sem("h"), sem("tp"), sem("hT")
        s_pj, s_pjr, s_rot, s_rh, s_rl = sem("pj"), sem("pj_read"), sem("rot"), sem("rh"), sem("rl")
        s_rp, s_ev = sem("replicated"), sem("replicated_read")
        s_qst = [sem(f"q_stored{g}") for g in range(NG)]
        block = ctx.enter_context(nc.Block())

        @block.sync
        def _(sp):
            sp.dma_start(ones[:], dram["ones_rows"]).then_inc(s_ones, 16)

            def load_rope(b):
                if b >= RB:
                    sp.wait_ge(s_pjr, 2 * (b - RB + 1))
                sp.dma_start(rope[:, b % RB], dram["rope"][:, :, b * BLK:(b + 1) * BLK]).then_inc(s_rope[b], 16)

            for b in range(RB):
                load_rope(b)
            for b in range(NB):
                for gi in range(NG):
                    sp.wait_ge(s_ev, (2 * b) * NG + gi + 1)
                    sp.dma_start(q_scratch[b, gi], f32(qs[:, gi, :])).then_inc(s_qst[gi], 16)
                if b + RB < NB:
                    load_rope(b + RB)
                if b == 0:
                    for g in range(3):
                        sp.wait_ge(s_qst[g], 16)
                        sp.wait_ge(s_zero, g + 1)
                        load_queries(sp, qm, s_qm, q_scratch, 0, g)
            for gi in range(NG):
                sp.wait_ge(s_qst[gi], 16 * NB)

        @block.gpsimd
        def _(pool):
            for g in range(NG):
                nc.gpsimd.memset(f32(qm[g][:]), 0.0).then_inc(s_zero, 1)

        @block.scalar
        def _(act):
            act.wait_ge(s_var, 1)
            nc.scalar.activation(small[:, 0, :], var[:], ACT.Sqrt).then_inc(s_sqrt, 1)
            act.wait_ge(s_ones, 16)
            for b in range(NB):
                act.wait_ge(s_tp, b + 1)
                nc.scalar.copy(hT[:, b * BLK:(b + 1) * BLK], rp[:, b, :]).then_inc(s_hT, 1)

            def high(J):
                act.wait_ge(s_rot, J + 1)
                if J >= 2:
                    act.wait_ge(s_rp, (J - 1) * NG)
                nc.scalar.copy(rh[:, J % 2, :], rr[:, J % 2, :]).then_inc(s_rh, 1)

            high(0)
            for b in range(NB):
                for j in range(2):
                    J = 2 * b + j
                    if J + 1 < 2 * NB:
                        high(J + 1)
                    for gi in range(NG):
                        act.wait_ge(s_rp, J * NG + gi + 1)
                        if j == 0:
                            if b:
                                act.wait_ge(s_qst[gi], 16 * b)
                            nc.scalar.copy(qs[:, gi, :], rp[:, gi, :]).then_inc(s_ev, 1)
                        else:
                            nc.scalar.activation(kr[:, gi, b * BLK:(b + 1) * BLK], rp[:, gi, :], ACT.Identity,
                                                 bias=ones[:, 0:1]).then_inc(s_ev, 1)

        @block.vector
        def _(dve):
            ch = Chain(dve, s_dve)
            inverse_deviation(nc, dve, ch, mv, var, small, s_var, s_sqrt)
            for b in range(NB):
                normalize_block(nc, x_tok, mv, small, h_tok, b, s_h)

            def rotate(J):
                b, j = J // 2, J % 2
                dve.wait_ge(s_rope[b], 16)
                dve.wait_ge(s_pj, J + 1)
                nc.vector.tensor_tensor(ra[:, j, :], pj[:, 2 * j, :], rope[:, b % RB, 0, :], ALU.mult)
                nc.vector.tensor_tensor(rbm[:, j, :], pj[:, 2 * j + 1, :], rope[:, b % RB, 1, :], ALU.mult).then_inc(s_pjr, 1)
                dve.wait_ge(s_pjr, J + 1)
                if J >= 2:
                    dve.wait_ge(s_rl, J - 1)
                nc.vector.tensor_tensor(rr[:, j, :], ra[:, j, :], rbm[:, j, :], ALU.add).then_inc(s_rot, 1)

            dve.wait_ge(s_tp, NB)
            rotate(0)
            for J in range(2 * NB):
                if J + 1 < 2 * NB:
                    rotate(J + 1)
                dve.wait_ge(s_rh, J + 1)
                if J >= 2:
                    dve.wait_ge(s_rp, (J - 1) * NG)
                nc.vector.tensor_tensor(rl[:, J % 2, :], rr[:, J % 2, :], f32(rh[:, J % 2, :]), ALU.subtract).then_inc(s_rl, 1)

        @block.tensor
        def _(pe):
            def project(J):
                b, j = J // 2, J % 2
                pe.wait_ge(s_hT, b + 1)
                if J >= 2:
                    pe.wait_ge(s_pjr, J - 1)
                for m in range(2):
                    w = slice((2 * j + m) * DIM, (2 * j + m + 1) * DIM)
                    mm = nc.tensor.matmul(pj[:, 2 * j + m, :], wqk[:, w], hT[:, b * BLK:(b + 1) * BLK], start=True, stop=True)
                mm.then_inc(s_pj, 1)

            for b in range(NB):
                pe.wait_ge(s_h, b + 1)
                transpose_block(nc, rp[:, b, :], h_tok, b, ident, s_tp)
                if b == 1:
                    project(0)
            project(1)
            pe.wait_ge(s_hT, NB)
            for J in range(2 * NB):
                j = J % 2
                if J + 2 < 2 * NB:
                    project(J + 2)
                pe.wait_ge(s_rl, J + 1)
                for gi in range(NG):
                    if J:
                        pe.wait_ge(s_ev, (J - 1) * NG + gi + 1)
                    w = slice(gi * P, (gi + 1) * P)
                    nc.tensor.matmul(rp[:, gi, :], sel[:, 2 * j, w], rh[:, j, :], start=True, stop=False)
                    mm = nc.tensor.matmul(rp[:, gi, :], sel[:, 2 * j + 1, w], rl[:, j, :], start=False, stop=True)
                    mm.then_inc(s_rp, 1)


def attention_phase(nc, dram, consts, x_tok, st, mv, kr, hT, wv, qm, s_qm, q_scratch):
    nm = "at_"
    ident, identr = consts["ident"], consts["identr"]
    STEPS = SEQ // P
    CHUNKS = SEQ // BLK
    MU = HG * TPB * CHUNKS
    PER = MU // STEPS
    LEAD = 3 * PER
    NGR = NB * NG
    RING = 3

    PROLOGUE = [("max", 0, u) for u in range(MU)] + [("max", 1, u) for u in range(PER)] + [("rows", 0, 0)]
    PROLOGUE += [("max", 1, u) for u in range(PER, LEAD)]
    WINDOW = [[("max", 1 + u // MU, u % MU) for u in range(LEAD + s * PER, LEAD + (s + 1) * PER)] for s in range(STEPS)]
    WINDOW[3].insert(0, ("acc", -1, 0))
    WINDOW[14].insert(0, ("rows", 1, 0))
    FLAT = [item for items in WINDOW for item in items]
    assert len(FLAT) % RING == 0
    O_BANK, X_BANK = (FLAT.index(("acc", -1, 0)) + 1) % RING, (FLAT.index(("acc", -1, 0)) + 2) % RING


    def place(item):
        return FLAT.index(item)

    with ExitStack() as ctx:
        def sb(name, shape, dt=F32):
            return ctx.enter_context(nc.sbuf_tensor(nm + name, shape, dt))

        def sem(name):
            return ctx.enter_context(nc.semaphore(nm + name))

        def pb(name, shape):
            return ctx.enter_context(nc.psum_tensor(nm + name + "_ps", shape, F32))

        v = sb("v", [P, NT, HEADS, VW])
        probs = sb("probs", [P, 4, 2 * BLK])
        mpart = sb("mpart", [P, 2, HG * TPB, CHUNKS])
        mx = sb("mx", [P, HG * TPB])
        mfull = sb("mfull", [P, TPB, P], F32R)
        mrows = sb("mrows", [P, BLK], F32R)
        acc_s = sb("acc_s", [P, BLK])
        rden = sb("rden", [P, TPB, HG])
        o_all = hT[:].rearrange("p (t d) -> p t d", d=DIM)
        oT = sb("oT", [P, BLK])
        wo, wob = sb("wo", [P, DIM]), sb("wob", [P, DIM])
        warm = sb("warm", [P, 1])
        st_ps = pb("st", [P, 2, 2 * BLK])
        ring = pb("ring", [P, RING, BLK])
        acc = pb("acc", [P, BLK])

        s_vp, s_ve, s_dve, s_fin = sem("v_done"), sem("v_copied"), sem("dve_chain"), sem("last_blocks")
        s_in, s_init = sem("in"), sem("init")
        s_mrow = sem("max_rows_stored")
        s_st, s_exp, s_pv = sem("scores"), sem("exp"), sem("pv")
        s_mx, s_red, s_mm = sem("max_scores"), sem("max_reduced"), sem("max_chain")
        s_mt, s_mr = sem("max_transposed"), sem("max_rows")
        s_accs, s_at, s_rd, s_o = sem("acc_copied"), sem("acc_transposed"), sem("rden"), sem("o")
        s_ot, s_oc, s_pr = sem("oT"), sem("oT_copied"), sem("projected")
        block = ctx.enter_context(nc.Block())

        def wait(eng, s, value):
            if not (isinstance(value, int) and value <= 0):
                eng.wait_ge(s, value)

        def groups(eng, group):
            group(0, 0, 0)
            with eng.Fori(0, NB - 1) as it:
                for k in range(1, NG + 1):
                    group(it * NG + k, k, it)
            for k in range(1, NG):
                group((NB - 1) * NG + k, k, NB - 1)

        def exists(G):
            return not isinstance(G, int) or G < NGR

        @block.sync
        def _(sp):
            for dst, src in ((wo[:], "wo"), (wob[:], "wob")):
                sp.dma_start(dst, dram[src]).then_inc(s_in, 16)

            def store_max_rows(k):
                for h in range(HG):
                    rows = slice(QUAD * h + ROW_M, QUAD * h + ROW_M + 2)
                    sp.dma_start(f32(qm[k % NG][rows, h, :]), f32(mrows[rows, :])).then_inc(s_mrow, 16)

            sp.wait_ge(s_mr, 1)
            store_max_rows(0)

            def group(G, k, it):
                if exists(G + 3):
                    wait(sp, s_st, G * 2 * STEPS)
                    load_queries(sp, qm, s_qm, q_scratch, it + (k + 3) // NG, (k + 3) % NG)
                if exists(G + 1):
                    sp.wait_ge(s_mr, G + 2)
                    store_max_rows(k + 1)

            groups(sp, group)

        @block.gpsimd
        def _(pool):
            nc.gpsimd.memset(f32(mfull[:]), 0.0).then_inc(s_init, 1)
            nc.gpsimd.memset(v[:, :, :, DK:VW], 1.0).then_inc(s_init, 1)

        @block.scalar
        def _(act):
            def copy_max_rows(G, bank):
                wait(act, s_mt, G + 1)
                wait(act, s_mrow, G * 64)
                nc.scalar.copy(mrows[:], ring[:, bank, :]).then_inc(s_mr, 1)

            def copy_acc(G):
                wait(act, s_pv, G * STEPS + STEPS)
                nc.scalar.copy(acc_s[:], acc[:]).then_inc(s_accs, 1)

            for b in range(NB):
                act.wait_ge(s_vp, b + 1)
                nc.scalar.copy(v[:, b * TPB:(b + 1) * TPB, :, 0:DK].rearrange("p t h d -> p (t h) d"),
                               st_ps[:, b // 2, b % 2 * BLK:(b % 2 + 1) * BLK].rearrange("p (n d) -> p n d", d=DK)).then_inc(s_ve, 1)
            copy_max_rows(0, (PROLOGUE.index(("rows", 0, 0)) - len(PROLOGUE)) % RING)

            def group(G, k, it):
                for s in range(STEPS):
                    T = G * STEPS + s
                    if s == 1 and k:
                        copy_acc(G - 1)
                    for pair in range(2):
                        if s == 14 and pair == 0 and exists(G + 1):
                            copy_max_rows(G + 1, place(("rows", 1, 0)) % RING)
                        act.wait_ge(s_st, T * 2 + pair + 1)
                        wait(act, s_pv, T - 1)
                        nc.scalar.activation(probs[:, 2 * (s % 2) + pair, :], st_ps[:, pair, :], ACT.Exp,
                                             scale=SCALE).then_inc(s_exp, 1)

            groups(act, group)
            nc.scalar.activation(warm[:], ident[:, 0:1], ACT.Sqrt)
            copy_acc(NGR - 1)

        @block.vector
        def _(dve):
            nc.vector.memset(acc[:], 0.0).then_inc(s_init, 1)

            def reduce_max(G, k, u, bank):
                V = G * MU + u
                if u == 0:
                    wait(dve, s_mm, G * 3 - 3)
                dve.wait_ge(s_mx, V + 1)
                nc.vector.tensor_reduce(mpart[:, k % 2, u // CHUNKS, u % CHUNKS:u % CHUNKS + 1], ring[:, bank, :], AX_X, ALU.max).then_inc(s_red, 1)

            def negate_max(G, k):
                dve.wait_ge(s_red, G * MU + MU)
                nc.vector.tensor_reduce(mx[:], mpart[:, k % 2], AX_X, ALU.max).then_inc(s_mm, 1)
                dve.wait_ge(s_mm, G * 3 + 1)
                wait(dve, s_mt, G)
                mf = mfull[:].rearrange("p t (h r) -> p t h r", r=QUAD)
                mq = mx[:].rearrange("p (h t) -> p t h", t=TPB)
                if isinstance(G, int) and G == 0:
                    dve.wait_ge(s_init, 3)
                nc.vector.tensor_scalar(mf[:, :, :, ROW_M], mq, -1.0, None, ALU.mult).then_inc(s_mm, 1)
                dve.wait_ge(s_mm, G * 3 + 2)
                nc.vector.scalar_tensor_tensor(out=mf[:, :, :, ROW_M + 1], in0=mq, scalar=-1.0,
                                               in1=f32(mfull[:]).rearrange("p t (h r) -> p t h r", r=QUAD)[:, :, :, ROW_M],
                                               op0=ALU.mult, op1=ALU.subtract).then_inc(s_mm, 1)

            def normalize(G, k, it):
                b, g = it + k // NG, k % NG
                dve.wait_ge(s_at, G + 1)
                m4 = ring[:, place(("acc", -1, 0)) % RING, :].rearrange("p (t h r) -> p t h r", t=TPB, r=QUAD)
                nc.vector.reciprocal(rden[:], m4[:, :, :, DK]).then_inc(s_rd, 1)
                dve.wait_ge(s_rd, G + 1)
                tiles = slice(b * TPB, (b + 1) * TPB) if isinstance(b, int) else bass.ds(b * TPB, TPB)
                out = o_all[:, tiles, g * HG * DK:(g + 1) * HG * DK].rearrange("p t (h d) -> p t h d", d=DK)
                nc.vector.tensor_tensor(out, m4[:, :, :, 0:DK], rden[:].unsqueeze(3).to_broadcast([P, TPB, HG, DK]),
                                        ALU.mult).then_inc(s_o, 1)

            ch = Chain(dve, s_dve)

            def finish_block(b):
                dve.wait_ge(s_ot, b + 1)
                nc.vector.tensor_copy(oT[:], ring[:, O_BANK, :]).then_inc(s_oc, 1)
                if b == 0:
                    dve.wait_ge(s_in, 32)
                xs = x_tok[:, b * TPB:(b + 1) * TPB, :]
                ch.link(nc.vector.tensor_tensor(xs, xs, wob[:].unsqueeze(1).to_broadcast([P, TPB, DIM]), ALU.add))
                dve.wait_ge(s_pr, b + 1)
                ch.link(nc.vector.tensor_tensor(xs, xs, ring[:, X_BANK, :].rearrange("p (t d) -> p t d", d=DIM), ALU.add))
                block_stats(nc, ch, x_tok, st, mv, b)

            for n, (kind, G, u) in enumerate(PROLOGUE, -len(PROLOGUE)):
                if kind == "max":
                    reduce_max(G, G, u, n % RING)
                    if (G, u) == (0, MU - 1):
                        negate_max(0, 0)

            def group(G, k, it):
                for s in range(STEPS):
                    for item in WINDOW[s]:
                        kind, ahead, u = item
                        if kind == "acc" and k:
                            normalize(G - 1, k - 1, it)
                        elif kind == "max" and exists(G + ahead):
                            reduce_max(G + ahead, k + ahead, u, place(item) % RING)
                            if u == MU - 1:
                                negate_max(G + 1, k + 1)
                    if isinstance(G, int) and G == NGR - 1 and (s - 5) % 3 == 0 and 0 <= s - 5 < 9:
                        finish_block((s - 5) // 3)

            groups(dve, group)
            normalize(NGR - 1, NG - 1, NB - 1)
            finish_block(NB - 1)

        @block.tensor
        def _(pe):
            def bank_free(G, n):
                while True:
                    n -= RING
                    if isinstance(G, int) and G * len(FLAT) + n < 0:
                        if n < -len(PROLOGUE):
                            return
                        kind, ahead, u = PROLOGUE[n]
                    else:
                        kind, ahead, u = FLAT[n % len(FLAT)]
                        ahead += n // len(FLAT)
                    if exists(G + ahead):
                        break
                if kind == "max":
                    pe.wait_ge(s_red, (G + ahead) * MU + u + 1)
                elif kind == "rows":
                    pe.wait_ge(s_mr, G + ahead + 1)
                else:
                    wait(pe, s_o, G + ahead + 1)

            def max_scores(G, k, it, u, bank):
                V, g = G * MU + u, k % NG
                h, t, c = u // (TPB * CHUNKS), u // CHUNKS % TPB, u % CHUNKS
                if u == 0:
                    pe.wait_ge(s_qm[g], 64 * (it + k // NG + 1))
                nc.tensor.matmul(ring[:, bank, :], qm[g][:, h, t * P:(t + 1) * P],
                                 kr[:, g, c * BLK:(c + 1) * BLK], start=True, stop=True).then_inc(s_mx, 1)

            def transpose_max(G, bank):
                pe.wait_ge(s_mm, G * 3 + 3)
                for t in range(TPB):
                    mm = nc.tensor.matmul(ring[:, bank, t * P:(t + 1) * P], mfull[:, t, :], identr[:], start=True, stop=True)
                mm.then_inc(s_mt, 1)

            def transpose_acc(G, bank):
                pe.wait_ge(s_accs, G + 1)
                for t in range(TPB):
                    mm = nc.tensor.transpose(ring[:, bank, t * P:(t + 1) * P], acc_s[:, t * P:(t + 1) * P], ident[:])
                mm.then_inc(s_at, 1)

            def scores(G, k, s, head):
                T, g, pair = G * STEPS + s, k % NG, head // 2
                if head % 2 == 0:
                    wait(pe, s_exp, T * 2 + pair - 1)
                mm = nc.tensor.matmul(st_ps[:, pair, head % 2 * BLK:(head % 2 + 1) * BLK], kr[:, g, s * P:(s + 1) * P],
                                      qm[g][:, head, :], start=True, stop=True)
                if head % 2:
                    mm.then_inc(s_st, 1)

            def values(G, k, s):
                g = k % NG
                pe.wait_ge(s_exp, G * 2 * STEPS + 2 * s + 2)
                if s == 0:
                    wait(pe, s_accs, G)
                for h in range(HG):
                    mm = nc.tensor.matmul(acc[QUAD * h:QUAD * h + VW, :], v[:, s, g * HG + h, :],
                                          probs[:, 2 * (s % 2) + h // 2, (h % 2) * BLK:(h % 2 + 1) * BLK],
                                          start=(s == 0), stop=(s == STEPS - 1), skip_group_check=True)
                mm.then_inc(s_pv, 1)

            def project_values(t):
                at = t % (NT // 2) * P
                mm = nc.tensor.matmul(st_ps[:, t // (NT // 2), at:at + P], hT[:, t * P:(t + 1) * P], wv[:],
                                      start=True, stop=True)
                if t % TPB == TPB - 1:
                    mm.then_inc(s_vp, 1)

            for n, (kind, G, u) in enumerate(PROLOGUE, -len(PROLOGUE)):
                bank_free(0, n)
                if kind == "max" and G == 0 and u % (MU // NT) == 0:
                    project_values(u // (MU // NT))
                if kind == "rows":
                    transpose_max(0, n % RING)
                else:
                    max_scores(G, G, 0, u, n % RING)
            pe.wait_ge(s_init, 3)
            pe.wait_ge(s_ve, NB)

            def group(G, k, it):
                for s in range(STEPS):
                    if s == 0:
                        pe.wait_ge(s_mrow, G * 64 + 64)
                    units = []
                    for item in WINDOW[s]:
                        kind, ahead, u = item
                        n = place(item)
                        if not exists(G + ahead) or (kind == "acc" and k == 0):
                            continue
                        if kind == "max":
                            units.append((ahead, u, n))
                            continue
                        bank_free(G, n)
                        if kind == "acc":
                            transpose_acc(G - 1, n % RING)
                        else:
                            transpose_max(G + 1, n % RING)
                    for head in range(HG):
                        scores(G, k, s, head)
                        for ahead, u, n in units[head:head + 1]:
                            bank_free(G, n)
                            max_scores(G + ahead, k + ahead, it, u, n % RING)
                    if s:
                        values(G, k, s - 1)
                    elif k:
                        values(G - 1, k - 1, STEPS - 1)
                    if isinstance(G, int) and G == NGR - 1 and 4 <= s < 13:
                        if (s - 4) % 3 == 0:
                            transpose_o((s - 4) // 3)
                        if (s - 4) % 3 == 1:
                            project_out((s - 4) // 3)

            def transpose_o(b):
                pe.wait_ge(s_o, (b + 1) * NG)
                if b == 0:
                    pe.wait_ge(s_in, 32)
                transpose_block(nc, ring[:, O_BANK, :], o_all, b, ident, s_ot)

            def project_out(b):
                pe.wait_ge(s_oc, b + 1)
                for t in range(TPB):
                    mm = nc.tensor.matmul(ring[:, X_BANK, t * P:(t + 1) * P], oT[:, t * P:(t + 1) * P], wo[:],
                                          start=True, stop=True)
                mm.then_inc(s_pr, 1)

            groups(pe, group)
            values(NGR - 1, NG - 1, STEPS - 1)
            bank_free(NGR, place(("acc", -1, 0)))
            transpose_acc(NGR - 1, place(("acc", -1, 0)) % RING)
            transpose_o(NB - 1)
            project_out(NB - 1)


def macaron_kernel(nc, dram):
    with ExitStack() as ctx:
        def sb(name, shape, dt=F32):
            return ctx.enter_context(nc.sbuf_tensor(name, shape, dt))

        x_tok = sb("x_tok", [P, NT, DIM])
        w1h, w1l = sb("w1h", [P, E * INNER], F32R), sb("w1l", [P, E * INNER], F32R)
        w2h, w2l = sb("w2h", [P, E * INNER], F32R), sb("w2l", [P, E * INNER], F32R)
        b2h, b2l = sb("b2h", [P, DIM], F32R), sb("b2l", [P, DIM], F32R)
        rw2 = sb("rw2", [P, P], F32R)
        consts = {
            "ident": sb("ident", [P, P]), "identr": sb("identr", [P, P], F32R),
            "onehot": sb("onehot", [P, E * P], F32R), "b1": sb("b1", [P, E * HALVES]), "rb": sb("rb", [2 * E, 1]),
        }
        weights = (w1h, w1l, w2h, w2l, b2h, b2l, rw2)
        st, mv = sb("st", [P, NT, 6]), sb("mv", [P, NT, 2])
        wqk, wv = sb("wqk", [P, 4 * DIM]), sb("wv", [P, DIM])
        sel = sb("sel", [P, 4, NG * P], F32R)
        q_scratch = nc.dram_tensor("q_scratch", [NB, NG, P, BLK], F32, kind="Internal").ap()
        ffn_phase(nc, "f1_", dram, consts, x_tok, st, mv, weights, first=True, ahead=(wqk, wv, sel))
        with ExitStack() as kv:
            kr = kv.enter_context(nc.sbuf_tensor("kr", [P, NG, SEQ], F32R))
            hT = kv.enter_context(nc.sbuf_tensor("hT", [P, SEQ], F32))
            qm = [kv.enter_context(nc.sbuf_tensor(f"qm{g}", [P, HG, BLK], F32R)) for g in range(NG)]
            s_qm = [kv.enter_context(nc.semaphore(f"queries_loaded{g}")) for g in range(NG)]
            project_phase(nc, dram, consts, x_tok, mv, kr, hT, wqk, sel, qm, s_qm, q_scratch)
            attention_phase(nc, dram, consts, x_tok, st, mv, kr, hT, wv, qm, s_qm, q_scratch)
        ffn_phase(nc, "f2_", dram, consts, x_tok, st, mv, weights, first=False)


def shape_constants(np):
    even, odd = np.arange(0, DIM, 2), np.arange(1, DIM, 2)
    pos = np.arange(SEQ, dtype=np.float32)
    freqs = np.exp(np.arange(0, DIM, 2, dtype=np.float32) * np.float32(-np.log(10000.0) / DIM)).astype(np.float32)
    ang = (freqs[:, None] * pos[None, :]).astype(np.float32)
    cos, sin = np.cos(ang), np.sin(ang)
    rope = np.stack([np.concatenate([cos, cos]), np.concatenate([-sin, sin])], axis=1).astype(np.float32)
    onehot = np.zeros((2 * E, E, P), np.float32)
    for e in range(E):
        onehot[e, e] = onehot[E + e, e] = 1.0
    sel = np.zeros((P, 4, NG, HG, QUAD), np.float32)
    rows = (((0, 2)), (1,), (0, 1), (2,))
    for f, thirds in enumerate(rows):
        for third in thirds:
            for g in range(NG):
                for h in range(HG):
                    for d in range(DK):
                        sel[(g * HG + h) * DK + d, f, g, h, third * DK + d] = 1.0
    ones_rows = np.zeros((HG, QUAD), np.float32)
    ones_rows[:, ROW_M:ROW_M + 2] = 1.0
    return {"rope": rope, "onehot": onehot.reshape(2 * E, E * P), "sel": sel.reshape(P, 4, NG * P),
            "ones_rows": ones_rows.reshape(P, 1), "ident": np.eye(P, dtype=np.float32),
            "perm_a": np.concatenate([even, odd]), "perm_b": np.concatenate([odd, even])}


def kernel(L0_attn_x, L0_attn_wq, L0_attn_wk, L0_attn_wv, L0_attn_wo_w, L0_attn_wo_b, L0_ffn_router_w,
           L0_ffn_router_b, L0_ffn_w1, L0_ffn_b1, L0_ffn_w2, L0_ffn_b2):
    import numpy as np
    import concourse.bacc as bacc
    from concourse.bass_utils import run_bass_kernel_spmd

    c = shape_constants(np)
    pa, pb = c.pop("perm_a"), c.pop("perm_b")
    wq, wk = np.asarray(L0_attn_wq), np.asarray(L0_attn_wk)
    arrays = {
        "x": np.asarray(L0_attn_x).reshape(SEQ, DIM),
        "wqk": np.concatenate([wq[pa].T, wq[pb].T, wk[pa].T, wk[pb].T], axis=1),
        "wv": np.asarray(L0_attn_wv).T, "wo": np.asarray(L0_attn_wo_w).T,
        "wob": np.broadcast_to(np.asarray(L0_attn_wo_b), (P, DIM)),
        "rw": np.asarray(L0_ffn_router_w), "rb": np.concatenate([np.asarray(L0_ffn_router_b), np.zeros(E, np.float32)]).reshape(2 * E, 1),
        "w1": np.asarray(L0_ffn_w1), "w2": np.asarray(L0_ffn_w2),
        "b1": np.asarray(L0_ffn_b1).reshape(E, HALVES, P).transpose(2, 0, 1).reshape(P, E * HALVES),
        "b2": np.concatenate([np.asarray(L0_ffn_b2)] * 2 + [np.zeros((P - 2 * E, DIM), np.float32)], axis=0),
        **c,
    }
    arrays = {n: np.ascontiguousarray(a) for n, a in arrays.items()}
    nc = bacc.Bacc("TRN2", target_bir_lowering=False, num_devices=1)
    dram = {n: nc.dram_tensor("in_" + n, a.shape, F32, kind="ExternalInput").ap() for n, a in arrays.items()}
    dram["out"] = nc.dram_tensor("out", (SEQ, DIM), F32, kind="ExternalOutput").ap()
    macaron_kernel(nc, dram)
    r = run_bass_kernel_spmd(nc, [{"in_" + n: a for n, a in arrays.items()}], core_ids=[0])
    return r.results[0]["out"].reshape(1, SEQ, DIM)
```

```python
from contextlib import ExitStack

import concourse.bass as bass
from concourse import mybir

F32 = mybir.dt.float32
F32R = mybir.dt.float32r
ALU = mybir.AluOpType
ACT = mybir.ActivationFunctionType
AX_X = mybir.AxisListType.X

P = 128
SEQ = 2048
DIM = 128
NT = SEQ // P
BLK = 512
NB = SEQ // BLK
TPB = BLK // P
E = 16
TOPK = 4
INNER = 256
HALVES = INNER // P
UNITS = E * HALVES
TURN = 10
HEADS = 16
DK = DIM // HEADS
HG = 4
NG = HEADS // HG
QUAD = 32
ROW_M = 3 * DK
VW = DK + 1
EPS = 1e-5
SCALE = DK ** -0.5


def f32(ap):
    return ap.bitcast(F32)


class Chain:

    def __init__(self, eng, sem):
        self.eng, self.sem, self.n = eng, sem, 0

    def link(self, ins):
        ins.then_inc(self.sem, 1)
        self.n += 1
        self.eng.wait_ge(self.sem, self.n)


def blocks_loop(eng, step):
    for u in range(TURN):
        step(0, u)
    with eng.Fori(0, NB - 1) as it:
        for u in range(TURN, UNITS):
            step(it, u)
        for u in range(TURN):
            step(it + 1, u)
    for u in range(TURN, UNITS):
        step(NB - 1, u)


def token_tile(tok, t):
    return tok[:, t, :] if isinstance(t, int) else tok[:, bass.ds(t, 1), :].squeeze(1)


def block_tiles(tok, b):
    return tok[:, b * TPB:(b + 1) * TPB, :] if isinstance(b, int) else tok[:, bass.ds(b * TPB, TPB), :]


def block_stats(nc, chain, x_tok, st, mv, b):
    for t in range(b * TPB, (b + 1) * TPB):
        last = nc.vector.bn_stats(st[:, t, :], x_tok[:, t, :])
    chain.link(last)
    for t in range(b * TPB, (b + 1) * TPB):
        last = nc.vector.bn_aggr(mv[:, t, :], st[:, t, :])
    chain.link(last)


def inverse_deviation(nc, dve, chain, mv, var, small, sem_var, sem_sqrt):
    nc.vector.tensor_scalar(var[:], mv[:, :, 1], EPS, None, ALU.add).then_inc(sem_var, 1)
    dve.wait_ge(sem_sqrt, 1)
    chain.link(nc.vector.reciprocal(small[:, 1, :], small[:, 0, :]))
    chain.link(nc.vector.tensor_tensor(small[:, 2, :], small[:, 1, :], small[:, 1, :], ALU.mult))
    chain.link(nc.vector.tensor_tensor(small[:, 3, :], small[:, 2, :], var[:], ALU.mult))
    chain.link(nc.vector.tensor_scalar(small[:, 2, :], small[:, 3, :], -0.5, 1.5, ALU.mult, ALU.add))
    chain.link(nc.vector.tensor_tensor(small[:, 4, :], small[:, 2, :], small[:, 1, :], ALU.mult))


def normalize_block(nc, x_tok, mv, small, h_tok, b, sem_h):
    for t in range(b * TPB, (b + 1) * TPB):
        last = nc.vector.tensor_scalar(h_tok[:, t, :], x_tok[:, t, :], mv[:, t, 0:1], small[:, 4, t:t + 1],
                                       ALU.subtract, ALU.mult)
    last.then_inc(sem_h, 1)


def transpose_block(nc, bank, tok, b, ident, sem):
    for t in range(TPB):
        last = nc.tensor.transpose(bank[:, t * P:(t + 1) * P], tok[:, b * TPB + t, :], ident[:])
    last.then_inc(sem, 1)


def ffn_phase(nc, nm, dram, consts, x_tok, st, mv, weights, c_scratch, first, ahead=None):
    w1h, w1l, w2h, w2l, b2h, b2l, rw2 = weights
    ident, identr, onehot, b1, rb = (consts[n] for n in ("ident", "identr", "onehot", "b1", "rb"))
    with ExitStack() as ctx:
        def sb(name, shape, dt=F32):
            return ctx.enter_context(nc.sbuf_tensor(nm + name, shape, dt))

        def pb(name, shape):
            return ctx.enter_context(nc.psum_tensor(nm + name + "_ps", shape, F32))

        def sem(name):
            return ctx.enter_context(nc.semaphore(nm + name))

        hh = sb("hh", [P, SEQ], F32R)
        hl = sb("hl", [P, SEQ], F32R)
        var, small = sb("var", [P, NT]), sb("small", [P, 5, NT])
        lg, ex, gt, eq, cs = (sb(n, [P, NT, E]) for n in ("lg", "ex", "gt", "eq", "cs"))
        first_e = sb("first_e", [P, NT, E])
        top8 = sb("top8", [P, NT, 8])
        tot, rtot = sb("tot", [P, NT]), sb("rtot", [P, NT])
        ct = sb("ct", [P, NT, E])
        c_all = sb("c_all", [P, 4, BLK])
        c2 = sb("c2", [P, NT, P])
        c2T = sb("c2T", [P, SEQ], F32R)
        g = sb("g", [P, 2, BLK])
        gc = sb("gc", [P, 4, BLK])
        gh, gl = sb("gh", [P, 4, BLK], F32R), sb("gl", [P, 4, BLK], F32R)
        h_tok = gc[:].rearrange("p a (t d) -> p (a t) d", d=DIM)
        yl = sb("y_or_logits", [P, SEQ])
        mv_b = sb("mv_b", [P, TPB, 2])
        warm = sb("warm", [P, 1])
        lT = yl[0:2 * E, :]
        cT = yl[2 * E:3 * E, :]
        yT = yl[:, 0:BLK]
        mid = pb("mid", [P, 4, BLK])
        cb = pb("cb", [P, 2, BLK])
        acc, aux = pb("acc", [P, BLK]), pb("aux", [P, BLK])
        c2_banks = (cb[:, 0, :], cb[:, 1, :], acc[:], aux[:])

        CH = 1024
        NCH = E * INNER // CH
        if first:
            w1f, w2f = sb("w1f", [P, E * INNER]), sb("w2f", [P, E * INNER])
            b2f, rwf = sb("b2f", [P, DIM]), sb("rwf", [P, E])
            s_x = [sem(f"x{b}") for b in range(NB)]
            s_small = sem("small_in")
            s_w = [[sem(f"w{m + 1}_{c}") for c in range(NCH)] for m in range(2)]
            s_hi, s_small_lo = sem("weights_hi"), sem("small_lo")
            s_wlo, s_rw, s_ahead = sem("weights_lo"), sem("router_zeros"), sem("loaded_ahead")
            wqk, wv = ahead
            onehot_in = yl[0:2 * E, :]
            s_stats, s_aggr = sem("stats"), sem("aggregated")
            s_tables, s_onehot, s_hi_last = sem("tables"), sem("onehot_loaded"), sem("weights_hi_last_chunk")
        if not first:
            s_out, s_out_last = sem("out"), sem("out_last")
        s_dve = sem("dve_chain")
        s_var, s_sqrt, s_h = sem("var"), sem("sqrt"), sem("h_tok")
        s_tp, s_hh, s_hl = sem("h_transposed"), sem("hh"), sem("hl")
        s_lg, s_lm, s_ex, s_c2 = sem("logits"), sem("logits_less_max"), sem("exp"), sem("c2")
        s_ctp, s_c2T = sem("c2_transposed"), sem("c2T")
        s_mid, s_gelu, s_cb, s_gc = sem("mid"), sem("gelu"), sem("cb"), sem("gc")
        s_ghi, s_glo, s_down, s_acc = sem("gh"), sem("gl"), sem("down"), sem("acc_copied")
        s_yt, s_xn = sem("y_transposed"), sem("x_new")
        s_lt, s_ltc, s_init = sem("logits_T"), sem("logits_T_copied"), sem("init")
        s_cT, s_c_stored = sem("cT"), sem("c_stored")
        s_c_all = [sem(f"c_spread{n}") for n in range(4)]
        SLOTS = 4
        block = ctx.enter_context(nc.Block())

        def store(eng, b, sem_out):
            eng.wait_ge(s_xn, b + 1)
            eng.dma_start(dram["out"].rearrange("(t p) d -> p t d", p=P)[:, b * TPB:(b + 1) * TPB, :],
                          x_tok[:, b * TPB:(b + 1) * TPB, :]).then_inc(sem_out, 16)

        def by_tensor_engine(b, u):
            return isinstance(b, int) and b == 0 and u < TURN

        @block.sync
        def _(sp):
            if first:
                xv = dram["x"].rearrange("(t p) d -> p t d", p=P)
                for b in range(NB):
                    sp.dma_start(x_tok[:, b * TPB:(b + 1) * TPB, :], xv[:, b * TPB:(b + 1) * TPB, :]).then_inc(s_x[b], 16)
                epc = CH // INNER
                for c in range(NCH):
                    sp.dma_start(w1f[:, c * CH:(c + 1) * CH].rearrange("p (e i) -> p e i", i=INNER),
                                 dram["w1"][c * epc:(c + 1) * epc].rearrange("e p i -> p e i")).then_inc(s_w[0][c], 16)
                    sp.dma_start(w2f[:, c * CH:(c + 1) * CH].rearrange("p (e t h) -> p e t h", t=HALVES, h=DIM),
                                 dram["w2"][c * epc:(c + 1) * epc].rearrange("e (t p) h -> p e t h", p=P)).then_inc(s_w[1][c], 16)
                for dst, src in ((wqk[:], "wqk"), (wv[:], "wv")):
                    sp.dma_start(dst, dram[src]).then_inc(s_ahead, 16)
                sp.wait_ge(s_ahead, 16 * 2)
            for b in range(NB):
                sp.wait_ge(s_cT, b + 1)
                sp.dma_start(c_scratch[b], cT[:, b * BLK:(b + 1) * BLK]).then_inc(s_c_stored, 16)
            sp.wait_ge(s_c_stored, 16 * NB)
            sp.sem_inc(s_c_all[0], 16)

            def step(b, u):
                e = u // HALVES
                if u % HALVES or by_tensor_engine(b, u):
                    return
                sp.wait_ge(s_gc, b * UNITS + u - 6)
                row = c_scratch[b, e] if isinstance(b, int) else c_scratch[bass.ds(b, 1), e].squeeze(0)
                sp.dma_start(c_all[:, e % 4, :], row.partition_broadcast(P)).then_inc(s_c_all[e % 4], 16)

            blocks_loop(sp, step)
            if not first:
                store(sp, NB - 1, s_out_last)
                sp.wait_ge(s_out_last, 16)

        @block.gpsimd
        def _(pool):
            if first:
                nc.gpsimd.memset(f32(onehot[:]), 0.0).then_inc(s_onehot, 1)
                pool.wait_ge(s_small, 16 * 5)
                pool.wait_ge(s_onehot, 16 + 1)
                nc.gpsimd.tensor_copy(onehot[0:2 * E, :], onehot_in).then_inc(s_tables, 1)
                nc.gpsimd.tensor_copy(identr[:], ident[:]).then_inc(s_tables, 1)
            nc.gpsimd.memset(c2[:], 0.0).then_inc(s_init, 1)
            nc.gpsimd.memset(first_e[:], 1.0).then_inc(s_init, 1)
            if not first:
                for b in range(NB - 1):
                    store(pool, b, s_out)
                pool.wait_ge(s_out, 16 * (NB - 1))
            if first:
                for c in range(NCH):
                    for m, (dst, src, hi) in enumerate(((w1l, w1f, w1h), (w2l, w2f, w2h))):
                        s = slice(c * CH, (c + 1) * CH)
                        if c == NCH - 1:
                            pool.wait_ge(s_w[m][c], 16)
                            nc.gpsimd.tensor_copy(hi[:, s], src[:, s]).then_inc(s_hi_last, 1)
                            pool.wait_ge(s_hi_last, m + 1)
                        else:
                            pool.wait_ge(s_hi, 2 + 2 * c + m + 1)
                        nc.gpsimd.tensor_tensor(dst[:, s], src[:, s], f32(hi[:, s]), ALU.subtract).then_inc(s_wlo, 1)

        @block.scalar
        def _(act):
            if first:
                for dst, src in ((ident[:], "ident"), (b1[:], "b1"), (rb[:], "rb"), (b2f[:], "b2"), (rwf[:], "rw")):
                    act.dma_start(dst, dram[src]).then_inc(s_small, 16)
                act.dma_start(onehot_in, dram["onehot"]).then_inc(s_onehot, 16)
                act.wait_ge(s_small, 16 * 5)
                act.wait_ge(s_rw, 1)
                for dst, src in ((rw2[:, 0:E], rwf[:]), (b2h[:], b2f[:])):
                    nc.scalar.copy(dst, src).then_inc(s_hi, 1)
            act.wait_ge(s_var, 1)
            nc.scalar.activation(small[:, 0, :], var[:], ACT.Sqrt).then_inc(s_sqrt, 1)
            if first:
                def split_high(c):
                    for m, (dst, src) in enumerate(((w1h, w1f), (w2h, w2f))):
                        act.wait_ge(s_w[m][c], 16)
                        nc.scalar.copy(dst[:, c * CH:(c + 1) * CH], src[:, c * CH:(c + 1) * CH]).then_inc(s_hi, 1)

                split_high(0)

            def copy_logits(b):
                if first and b == 0:
                    act.wait_ge(s_tables, 1)
                act.wait_ge(s_lt, b + 1)
                nc.scalar.activation(lT[:, b * BLK:(b + 1) * BLK], cb[0:2 * E, b % 2, :],
                                     ACT.Identity, bias=rb[0:2 * E, 0:1]).then_inc(s_ltc, 1)

            for b in range(NB):
                act.wait_ge(s_tp, b + 1)
                nc.scalar.copy(hh[:, b * BLK:(b + 1) * BLK], mid[:, b, :]).then_inc(s_hh, 1)
                if b:
                    copy_logits(b - 1)
            copy_logits(NB - 1)
            if first:
                split_high(1)
            act.wait_ge(s_lm, 1)
            nc.scalar.activation(ex[:], lg[:], ACT.Exp).then_inc(s_ex, 1)
            if first:
                split_high(2)

            act.sem_inc(s_gelu, SLOTS)
            act.sem_inc(s_acc, 1)

            def gelu(b, u):
                act.wait_ge(s_mid, b * UNITS + u + 1)
                nc.scalar.activation(g[:, u % 2, :], mid[:, u % 4, :], ACT.Gelu,
                                     bias=b1[:, u % UNITS:u % UNITS + 1]).then_inc(s_gelu, 1)

            def copy_c2T(b):
                act.wait_ge(s_ctp, b + 1)
                nc.scalar.copy(cT[:, b * BLK:(b + 1) * BLK], c2_banks[b][2 * E:3 * E, :]).then_inc(s_cT, 1)
                nc.scalar.copy(c2T[:, b * BLK:(b + 1) * BLK], c2_banks[b]).then_inc(s_c2T, 1)

            def step(b, u):
                if not (isinstance(b, int) and (b, u) in ((0, 0), (NB - 1, UNITS - 1))):
                    gelu(b, u + 1)
                act.wait_ge(s_gc, b * UNITS + u + 1)
                act.wait_ge(s_down, b * UNITS + u + 1)
                nc.scalar.copy(gh[:, u % 4, :], gc[:, u % 4, :]).then_inc(s_ghi, 1)
                if isinstance(b, int) and b == 0:
                    if u + 2 < NB:
                        copy_c2T(u + 2)
                    if u == TURN - 1:
                        act.wait_ge(s_c_stored, 16 * NB)
                elif u == 1:
                    copy_acc(b - 1)

            def copy_acc(b):
                act.wait_ge(s_down, SLOTS + (b + 1) * UNITS)
                nc.scalar.copy(yT, acc[:]).then_inc(s_acc, 1)

            gelu(0, 0)
            gelu(0, 1)
            copy_c2T(0)
            copy_c2T(1)
            blocks_loop(act, step)
            if first:
                nc.scalar.activation(warm[:], ident[:, 0:1], ACT.Sqrt)
            copy_acc(NB - 1)

        @block.vector
        def _(dve):
            ch = Chain(dve, s_dve)
            if first:
                nc.vector.memset(f32(rw2[:]), 0.0).then_inc(s_rw, 1)
                for b in range(NB):
                    dve.wait_ge(s_x[b], 16)
                    block_stats(nc, ch, x_tok, st, mv, b)
            if first:
                dve.wait_ge(s_hi, 2)
                nc.vector.tensor_tensor(rw2[:, E:2 * E], rwf[:], f32(rw2[:, 0:E]), ALU.subtract).then_inc(s_small_lo, 1)
                nc.vector.tensor_tensor(b2l[:], b2f[:], f32(b2h[:]), ALU.subtract).then_inc(s_small_lo, 1)
            inverse_deviation(nc, dve, ch, mv, var, small, s_var, s_sqrt)
            normalize_block(nc, x_tok, mv, small, h_tok, 0, s_h)
            for b in range(NB):
                if b + 1 < NB:
                    normalize_block(nc, x_tok, mv, small, h_tok, b + 1, s_h)
                dve.wait_ge(s_hh, b + 1)
                s = slice(b * BLK, (b + 1) * BLK)
                nc.vector.tensor_tensor(hl[:, s], mid[:, b, :], f32(hh[:, s]), ALU.subtract).then_inc(s_hl, 1)
            dve.wait_ge(s_init, 2)
            ch.link(nc.vector.memset(first_e[:, :, 0:1], 0.0))
            dve.wait_ge(s_lg, 1)
            ch.link(nc.vector.tensor_reduce(lg[:], acc[:].rearrange("p (t s e) -> p t e s", s=2, e=E), AX_X, ALU.add))
            for t in range(NT):
                last = nc.vector.max(top8[:, t, :], lg[:, t, :])
            ch.link(last)
            thr = top8[:, :, TOPK - 1:TOPK].to_broadcast([P, NT, E])
            nc.vector.tensor_tensor(gt[:], lg[:], thr, ALU.is_gt)
            ch.link(nc.vector.tensor_tensor(eq[:], lg[:], thr, ALU.is_equal))
            nc.vector.tensor_tensor(lg[:], lg[:], top8[:, :, 0:1].to_broadcast([P, NT, E]),
                                    ALU.subtract).then_inc(s_lm, 1)
            flat = "p t e -> p (t e)"
            nc.vector.tensor_tensor_scan(cs[:].rearrange(flat), first_e[:].rearrange(flat), eq[:].rearrange(flat), 0.0,
                                         ALU.mult, ALU.add)
            ch.link(nc.vector.tensor_reduce(tot[:], gt[:], AX_X, ALU.add))
            ch.link(nc.vector.scalar_tensor_tensor(out=ct[:], in0=cs[:], scalar=-float(TOPK),
                                                   in1=tot[:].unsqueeze(2).to_broadcast([P, NT, E]),
                                                   op0=ALU.add, op1=ALU.add))
            ch.link(nc.vector.scalar_tensor_tensor(out=eq[:], in0=ct[:], scalar=0.0, in1=eq[:], op0=ALU.is_le, op1=ALU.mult))
            ch.link(nc.vector.tensor_tensor(gt[:], gt[:], eq[:], ALU.add))
            dve.wait_ge(s_ex, 1)
            ch.link(nc.vector.tensor_tensor(ex[:], ex[:], gt[:], ALU.mult))
            ch.link(nc.vector.tensor_reduce(tot[:], ex[:], AX_X, ALU.add))
            ch.link(nc.vector.reciprocal(rtot[:], tot[:]))
            cw, c_hi, c_lo = c2[:, :, 2 * E:3 * E], c2[:, :, 0:E], c2[:, :, E:2 * E]
            ch.link(nc.vector.scalar_tensor_tensor(out=cw, in0=ex[:], scalar=0.5,
                                                   in1=rtot[:].unsqueeze(2).to_broadcast([P, NT, E]),
                                                   op0=ALU.mult, op1=ALU.mult))
            ch.link(nc.vector.tensor_copy(c_hi.bitcast(F32R), cw))
            nc.vector.tensor_tensor(c_lo.bitcast(F32R), cw, c_hi, ALU.subtract).then_inc(s_c2, 1)

            dve.sem_inc(s_glo, SLOTS)

            def gate(b, u):
                U = b * UNITS + u
                dve.wait_ge(s_gelu, U + 1 + SLOTS)
                e = u // HALVES
                if by_tensor_engine(b, u):
                    dve.wait_ge(s_cb, e + 1)
                    spread_c = cb[:, e % 2, :]
                else:
                    dve.wait_ge(s_c_all[e % 4], 16 * (b * (E // 4) + e // 4))
                    spread_c = c_all[:, e % 4, :]
                dve.wait_ge(s_glo, U + 1)
                nc.vector.tensor_tensor(gc[:, u % 4, :], g[:, u % 2, :], spread_c, ALU.mult).then_inc(s_gc, 1)

            def step(b, u):
                if not (isinstance(b, int) and (b, u) == (NB - 1, UNITS - 1)):
                    gate(b, u + 1)
                U = b * UNITS + u
                finishing = not (isinstance(b, int) and b == 0) and u in FINISH
                if finishing:
                    finish_wait(b - 1, FINISH.index(u))
                dve.wait_ge(s_ghi, U + 1)
                dve.wait_ge(s_down, U + 1)
                nc.vector.tensor_tensor(gl[:, u % 4, :], gc[:, u % 4, :], f32(gh[:, u % 4, :]),
                                        ALU.subtract).then_inc(s_glo, 1)
                if finishing:
                    finish(b - 1, FINISH.index(u))

            FINISH = (5, 6, 7, 9)

            def finish_wait(b, part):
                if part == 0:
                    dve.wait_ge(s_yt, b + 1)
                elif first:
                    dve.wait_ge((s_xn, s_stats, s_aggr)[part - 1], b + 1)

            def finish(b, part):
                if part == 0:
                    nc.vector.tensor_tensor(block_tiles(x_tok, b), block_tiles(x_tok, b), aux[:].rearrange("p (t d) -> p t d", d=DIM),
                                            ALU.add).then_inc(s_xn, 1)
                elif first:
                    if part == 3:
                        nc.vector.tensor_copy(block_tiles(mv, b), mv_b[:])
                        return
                    for t in range(TPB):
                        if part == 1:
                            last = nc.vector.bn_stats(st[:, t, :], token_tile(x_tok, b * TPB + t))
                        else:
                            last = nc.vector.bn_aggr(mv_b[:, t, :], st[:, t, :])
                    last.then_inc((s_stats, s_aggr)[part - 1], 1)

            gate(0, 0)
            blocks_loop(dve, step)
            for part in range(len(FINISH)):
                finish_wait(NB - 1, part)
                finish(NB - 1, part)

        @block.tensor
        def _(pe):
            if first:
                pe.wait_ge(s_small, 16 * 5)

            def transpose_h(b):
                pe.wait_ge(s_h, b + 1)
                transpose_block(nc, mid[:, b, :], h_tok, b, ident, s_tp)

            def logits(b):
                pe.wait_ge(s_hl, b + 1)
                if b >= 2:
                    pe.wait_ge(s_ltc, b - 1)
                s = slice(b * BLK, (b + 1) * BLK)
                nc.tensor.matmul(cb[:, b % 2, :], rw2[:], hh[:, s], start=True, stop=False)
                nc.tensor.matmul(cb[:, b % 2, :], rw2[:], hl[:, s], start=False, stop=True).then_inc(s_lt, 1)

            def logits_to_tokens(b):
                pe.wait_ge(s_ltc, b + 1)
                for t in range(b * TPB, (b + 1) * TPB):
                    last = nc.tensor.transpose(acc[:, t * 2 * E:(t + 1) * 2 * E], lT[:, t * P:(t + 1) * P],
                                               ident[0:2 * E, 0:2 * E])
                if b == NB - 1:
                    last.then_inc(s_lg, 1)

            transpose_h(0)
            transpose_h(1)
            if first:
                pe.wait_ge(s_small_lo, 1)
            for b in range(NB):
                logits(b)
                if b + 2 < NB:
                    transpose_h(b + 2)
                if b:
                    logits_to_tokens(b - 1)
            logits_to_tokens(NB - 1)

            def mids(b, u):
                e, half = u % UNITS // HALVES, u % HALVES
                U = b * UNITS + u
                if not (isinstance(U, int) and U < 4):
                    pe.wait_ge(s_gelu, U + 1)
                w = slice(e * INNER + half * P, e * INNER + (half + 1) * P)
                if first and u < UNITS and w.start % CH == 0:
                    pe.wait_ge(s_wlo, 2 * (w.start // CH) + 1)
                ts = bass.ts(b + u // UNITS, BLK)
                for n, (wp, hp) in enumerate(((w1h, hh), (w1h, hl), (w1l, hh))):
                    mm = nc.tensor.matmul(mid[:, u % 4, :], wp[:, w], hp[:, ts], start=(n == 0), stop=(n == 2))
                mm.then_inc(s_mid, 1)

            def spread(e):
                if e >= 2:
                    pe.wait_ge(s_gc, 2 * e - 2)
                nc.tensor.matmul(cb[:, e % 2, :], onehot[:, e * P:(e + 1) * P], c2T[:, 0:BLK],
                                 start=True, stop=True).then_inc(s_cb, 1)

            for u in range(3):
                mids(0, u)
            pe.wait_ge(s_c2, 1)
            if first:
                pe.wait_ge(s_tables, 2)
            for b in range(NB):
                for t in range(TPB):
                    mm = nc.tensor.transpose(c2_banks[b][:, t * P:(t + 1) * P], c2[:, b * TPB + t, :], ident[:])
                mm.then_inc(s_ctp, 1)
                if b in (1, 2):
                    pe.wait_ge(s_c2T, b)
                    spread(b - 1)
            if first:
                pe.wait_ge(s_small_lo, 2)
            pe.sem_inc(s_down, SLOTS)
            LEAD = 3

            def step(b, u):
                last = isinstance(b, int) and b == NB - 1
                if not (last and u + LEAD >= UNITS):
                    mids(b, u + LEAD)
                    if (u + LEAD) % HALVES == 0 and by_tensor_engine(b, u + LEAD):
                        spread((u + LEAD) // HALVES)
                e, half = u // HALVES, u % HALVES
                if u == 0:
                    if isinstance(b, int) and b == 0:
                        pe.wait_ge(s_c2T, NB - 1)
                    pe.wait_ge(s_acc, b + 1)
                    for n, b2 in enumerate((b2h, b2l)):
                        nc.tensor.matmul(acc[:], b2[:], c2T[:, bass.ts(b, BLK)], start=(n == 0), stop=False)
                pe.wait_ge(s_glo, b * UNITS + u + 1 + SLOTS)
                w = slice((e * HALVES + half) * DIM, (e * HALVES + half + 1) * DIM)
                if first and w.start % CH == 0:
                    pe.wait_ge(s_wlo, 2 * (w.start // CH) + 2)
                for n, (wp, gp) in enumerate(((w2h, gh), (w2h, gl), (w2l, gh))):
                    mm = nc.tensor.matmul(acc[:], wp[:, w], gp[:, u % 4, :], start=False,
                                          stop=(u == UNITS - 1 and n == 2))
                mm.then_inc(s_down, 1)
                if u == 3:
                    if isinstance(b, int) and b == 0:
                        pe.wait_ge(s_c2T, NB)
                    else:
                        transpose_y(b - 1)

            def transpose_y(b):
                pe.wait_ge(s_acc, b + 2)
                for t in range(TPB):
                    mm = nc.tensor.transpose(aux[:, t * P:(t + 1) * P], yT[:, t * P:(t + 1) * P], ident[:])
                mm.then_inc(s_yt, 1)

            blocks_loop(pe, step)
            transpose_y(NB - 1)


def load_queries(sp, qm, s_qm, q_scratch, b, g):
    for h in range(HG):
        rows = slice(QUAD * h, QUAD * (h + 1))
        src = q_scratch[b, g, rows] if isinstance(b, int) else q_scratch[bass.ds(b, 1), g, rows].squeeze(0)
        sp.dma_start(f32(qm[g][rows, h, :]), src).then_inc(s_qm[g], 16)


def project_phase(nc, dram, consts, x_tok, mv, kr, hT, wqk, sel, qm, s_qm, q_scratch):
    nm = "pr_"
    ident = consts["ident"]
    with ExitStack() as ctx:
        def sb(name, shape, dt=F32):
            return ctx.enter_context(nc.sbuf_tensor(nm + name, shape, dt))

        def sem(name):
            return ctx.enter_context(nc.semaphore(nm + name))

        work = sb("work", [P, 4, BLK])
        h_tok = work[:].rearrange("p a (t d) -> p (a t) d", d=DIM)
        ra, rbm = work[:, 0:2, :], work[:, 2:4, :]
        var, small = sb("var", [P, NT]), sb("small", [P, 5, NT])
        RB = 3
        rope = sb("rope", [P, RB, 2, BLK])
        ones = sb("ones_rows", [P, 1])
        rr = sb("rot", [P, 2, BLK])
        rh, rl = sb("rot_hi", [P, 2, BLK], F32R), sb("rot_lo", [P, 2, BLK], F32R)
        qs = sb("qs", [P, 4, BLK], F32R)
        pj = ctx.enter_context(nc.psum_tensor(nm + "pj", [P, 4, BLK], F32))
        rp = ctx.enter_context(nc.psum_tensor(nm + "rp", [P, 4, BLK], F32))
        s_ones, s_zero, s_dve = sem("ones_loaded"), sem("zeros"), sem("dve_chain")
        s_rope = [sem(f"rope{b}") for b in range(NB)]
        s_sel_in, s_sel = [sem(f"sel_loaded{f}") for f in range(4)], sem("sel")
        s_var, s_sqrt, s_h, s_tp, s_hT = sem("var"), sem("sqrt"), sem("h"), sem("tp"), sem("hT")
        s_pj, s_pjr, s_rot, s_rh, s_rl = sem("pj"), sem("pj_read"), sem("rot"), sem("rh"), sem("rl")
        s_rp, s_ev = sem("replicated"), sem("replicated_read")
        s_qst = [sem(f"q_stored{g}") for g in range(NG)]
        block = ctx.enter_context(nc.Block())
        JOBS = [(0, 1), (0, 0), (1, 1), (2, 1), (3, 1)]
        QUERIES = JOBS.index((0, 0))

        @block.sync
        def _(sp):
            for f in range(4):
                sp.dma_start(f32(qs[:, f, :]), dram["sel"][:, f, :]).then_inc(s_sel_in[f], 16)
            sp.dma_start(ones[:], dram["ones_rows"]).then_inc(s_ones, 16)

            def load_rope(b):
                if b == RB:
                    sp.wait_ge(s_pjr, 2)
                sp.dma_start(rope[:, b % RB], dram["rope"][:, :, b * BLK:(b + 1) * BLK]).then_inc(s_rope[b], 16)

            for b in range(RB):
                load_rope(b)
            load_rope(RB)
            for gi in range(NG):
                sp.wait_ge(s_ev, QUERIES * NG + gi + 1)
                sp.dma_start(q_scratch[0, gi], f32(qs[:, gi, :])).then_inc(s_qst[gi], 16)
            for g in range(3):
                sp.wait_ge(s_qst[g], 16)
                sp.wait_ge(s_zero, g + 1)
                load_queries(sp, qm, s_qm, q_scratch, 0, g)
            sp.wait_ge(s_qst[3], 16)

        @block.gpsimd
        def _(pool):
            for f in range(4):
                pool.wait_ge(s_sel_in[f], 16)
                nc.gpsimd.tensor_copy(sel[:, f, :], f32(qs[:, f, :])).then_inc(s_sel, 1)
            for g in range(NG):
                nc.gpsimd.memset(f32(qm[g][:]), 0.0).then_inc(s_zero, 1)

        @block.scalar
        def _(act):
            act.wait_ge(s_var, 1)
            nc.scalar.activation(small[:, 0, :], var[:], ACT.Sqrt).then_inc(s_sqrt, 1)
            act.wait_ge(s_ones, 16)
            for b in range(NB):
                act.wait_ge(s_tp, b + 1)
                nc.scalar.copy(hT[:, b * BLK:(b + 1) * BLK], rp[:, b, :]).then_inc(s_hT, 1)

            def high(J):
                act.wait_ge(s_rot, J + 1)
                if J >= 2:
                    act.wait_ge(s_rp, (J - 1) * NG)
                nc.scalar.copy(rh[:, J % 2, :], rr[:, J % 2, :]).then_inc(s_rh, 1)

            high(0)
            for J, (b, j) in enumerate(JOBS):
                if J + 1 < len(JOBS):
                    high(J + 1)
                for gi in range(NG):
                    act.wait_ge(s_rp, J * NG + gi + 1)
                    if j == 0:
                        nc.scalar.copy(qs[:, gi, :], rp[:, gi, :]).then_inc(s_ev, 1)
                    else:
                        nc.scalar.activation(kr[:, gi, b * BLK:(b + 1) * BLK], rp[:, gi, :], ACT.Identity,
                                             bias=ones[:, 0:1]).then_inc(s_ev, 1)

        @block.vector
        def _(dve):
            ch = Chain(dve, s_dve)
            inverse_deviation(nc, dve, ch, mv, var, small, s_var, s_sqrt)
            for b in range(NB):
                normalize_block(nc, x_tok, mv, small, h_tok, b, s_h)

            def rotate(J):
                b, n = JOBS[J][0], J % 2
                dve.wait_ge(s_rope[b], 16)
                dve.wait_ge(s_pj, J + 1)
                nc.vector.tensor_tensor(ra[:, n, :], pj[:, 2 * n, :], rope[:, b % RB, 0, :], ALU.mult)
                nc.vector.tensor_tensor(rbm[:, n, :], pj[:, 2 * n + 1, :], rope[:, b % RB, 1, :], ALU.mult).then_inc(s_pjr, 1)
                dve.wait_ge(s_pjr, J + 1)
                if J >= 2:
                    dve.wait_ge(s_rl, J - 1)
                nc.vector.tensor_tensor(rr[:, n, :], ra[:, n, :], rbm[:, n, :], ALU.add).then_inc(s_rot, 1)

            dve.wait_ge(s_tp, NB)
            rotate(0)
            for J in range(len(JOBS)):
                if J + 1 < len(JOBS):
                    rotate(J + 1)
                dve.wait_ge(s_rh, J + 1)
                if J >= 2:
                    dve.wait_ge(s_rp, (J - 1) * NG)
                nc.vector.tensor_tensor(rl[:, J % 2, :], rr[:, J % 2, :], f32(rh[:, J % 2, :]), ALU.subtract).then_inc(s_rl, 1)

        @block.tensor
        def _(pe):
            def project(J):
                (b, j), n = JOBS[J], J % 2
                pe.wait_ge(s_hT, b + 1)
                if J >= 2:
                    pe.wait_ge(s_pjr, J - 1)
                for m in range(2):
                    w = slice((2 * j + m) * DIM, (2 * j + m + 1) * DIM)
                    mm = nc.tensor.matmul(pj[:, 2 * n + m, :], wqk[:, w], hT[:, b * BLK:(b + 1) * BLK], start=True, stop=True)
                mm.then_inc(s_pj, 1)

            for b in range(NB):
                pe.wait_ge(s_h, b + 1)
                transpose_block(nc, rp[:, b, :], h_tok, b, ident, s_tp)
                if b == 1:
                    project(0)
            project(1)
            pe.wait_ge(s_hT, NB)
            pe.wait_ge(s_sel, 4)
            for J, (_, j) in enumerate(JOBS):
                if J + 2 < len(JOBS):
                    project(J + 2)
                pe.wait_ge(s_rl, J + 1)
                for gi in range(NG):
                    if J:
                        pe.wait_ge(s_ev, (J - 1) * NG + gi + 1)
                    w = slice(gi * P, (gi + 1) * P)
                    nc.tensor.matmul(rp[:, gi, :], sel[:, 2 * j, w], rh[:, J % 2, :], start=True, stop=False)
                    mm = nc.tensor.matmul(rp[:, gi, :], sel[:, 2 * j + 1, w], rl[:, J % 2, :], start=False, stop=True)
                    mm.then_inc(s_rp, 1)


def attention_phase(nc, dram, consts, x_tok, st, mv, kr, hT, wqk, wv, sel, qm, s_qm, q_scratch):
    nm = "at_"
    ident, identr = consts["ident"], consts["identr"]
    STEPS = SEQ // P
    CHUNKS = SEQ // BLK
    MU = HG * TPB * CHUNKS
    PER = MU // STEPS
    LEAD = 3 * PER
    NGR = NB * NG
    RING = 3

    PROLOGUE = [("max", 0, u) for u in range(MU)] + [("max", 1, u) for u in range(PER)] + [("rows", 0, 0)]
    PROLOGUE += [("max", 1, u) for u in range(PER, LEAD)]
    WINDOW = [[("max", 1 + u // MU, u % MU) for u in range(LEAD + s * PER, LEAD + (s + 1) * PER)] for s in range(STEPS)]
    WINDOW[3].insert(0, ("acc", -1, 0))
    WINDOW[14].insert(0, ("rows", 1, 0))
    FLAT = [item for items in WINDOW for item in items]
    assert len(FLAT) % RING == 0
    O_BANK, X_BANK = (FLAT.index(("acc", -1, 0)) + 1) % RING, (FLAT.index(("acc", -1, 0)) + 2) % RING


    def place(item):
        return FLAT.index(item)

    BESIDE = {("v", u): u // TPB for u in range(0, MU, TPB)}
    for b in range(1, NB):
        u = (b - 1) * 16
        BESIDE.update({("project", u + at): 4 * (b - 1) + n for n, at in enumerate((1, 2, 3, 5))})
        BESIDE.update({("raw", u + 6): b, ("high", u + 12): b})
        BESIDE.update({("row", u + 20 + 3 * g): (b - 1) * NG + g for g in range(NG)})

    def beside(u, kind):
        return BESIDE.get((kind, u))

    with ExitStack() as ctx:
        def sb(name, shape, dt=F32):
            return ctx.enter_context(nc.sbuf_tensor(nm + name, shape, dt))

        def sem(name):
            return ctx.enter_context(nc.semaphore(nm + name))

        def pb(name, shape):
            return ctx.enter_context(nc.psum_tensor(nm + name + "_ps", shape, F32))

        v = sb("v", [P, NT, HEADS, VW])
        probs = sb("probs", [P, 4, 2 * BLK])
        rot_hi, rot_lo = sb("rot_hi", [P, BLK], F32R), sb("rot_lo", [P, BLK], F32R)
        mpart = sb("mpart", [P, 2, HG * TPB, CHUNKS])
        mx = sb("mx", [P, HG * TPB])
        mfull = sb("mfull", [P, TPB, P], F32R)
        mrows = sb("mrows", [P, BLK], F32R)
        acc_s = sb("acc_s", [P, BLK])
        rden = sb("rden", [P, TPB, HG])
        o_all = hT[:].rearrange("p (t d) -> p t d", d=DIM)
        oT = sb("oT", [P, BLK])
        wo, wob = sb("wo", [P, DIM]), sb("wob", [P, DIM])
        warm = sb("warm", [P, 1])
        st_ps = pb("st", [P, 2, 2 * BLK])
        ring = pb("ring", [P, RING, BLK])
        acc = pb("acc", [P, BLK])

        s_vp, s_ve, s_dve = sem("v_done"), sem("v_copied"), sem("dve_chain")
        rope = [probs[:, b - 1, :].rearrange("p (m c) -> p m c", c=BLK) for b in range(1, NB)]
        raw = probs[:, NB - 1, :].rearrange("p (m c) -> p m c", c=BLK)
        qs = (acc_s, oT)
        s_rope, s_qpj, s_raw = [sem(f"rope{b}") for b in range(1, NB)], sem("q_projected"), sem("q_copied")
        s_pool, s_rot, s_rh, s_rl = sem("gpsimd_chain"), sem("rot"), sem("rot_hi"), sem("rot_lo")
        s_rp, s_ev, s_qst = sem("replicated"), sem("replicated_read"), [sem(f"q_stored{n}") for n in range(2)]
        s_in, s_init = sem("in"), sem("init")
        s_mrow = sem("max_rows_stored")
        s_st, s_exp, s_pv = sem("scores"), sem("exp"), sem("pv")
        s_mx, s_red, s_mm = sem("max_scores"), sem("max_reduced"), sem("max_chain")
        s_mt, s_mr = sem("max_transposed"), sem("max_rows")
        s_accs, s_at, s_rd, s_o = sem("acc_copied"), sem("acc_transposed"), sem("rden"), sem("o")
        s_ot, s_oc, s_pr = sem("oT"), sem("oT_copied"), sem("projected")
        block = ctx.enter_context(nc.Block())

        def wait(eng, s, value):
            if not (isinstance(value, int) and value <= 0):
                eng.wait_ge(s, value)

        def groups(eng, group):
            group(0, 0, 0)
            with eng.Fori(0, NB - 1) as it:
                for k in range(1, NG + 1):
                    group(it * NG + k, k, it)
            for k in range(1, NG):
                group((NB - 1) * NG + k, k, NB - 1)

        def exists(G):
            return not isinstance(G, int) or G < NGR

        @block.sync
        def _(sp):
            for b in range(1, NB):
                sp.dma_start(rope[b - 1], dram["rope"][:, :, b * BLK:(b + 1) * BLK]).then_inc(s_rope[b - 1], 16)
            for dst, src in ((wo[:], "wo"), (wob[:], "wob")):
                sp.dma_start(dst, dram[src]).then_inc(s_in, 16)
            for n in range((NB - 1) * NG):
                sp.wait_ge(s_ev, n + 1)
                sp.dma_start(q_scratch[1 + n // NG, n % NG], qs[n % 2][:]).then_inc(s_qst[n % 2], 16)
            for n in range(2):
                sp.wait_ge(s_qst[n], 16 * (NB - 1) * NG // 2)

            def store_max_rows(k):
                for h in range(HG):
                    rows = slice(QUAD * h + ROW_M, QUAD * h + ROW_M + 2)
                    sp.dma_start(f32(qm[k % NG][rows, h, :]), f32(mrows[rows, :])).then_inc(s_mrow, 16)

            sp.wait_ge(s_mr, 1)
            store_max_rows(0)

            def group(G, k, it):
                if exists(G + 3):
                    wait(sp, s_st, G * 2 * STEPS)
                    load_queries(sp, qm, s_qm, q_scratch, it + (k + 3) // NG, (k + 3) % NG)
                if exists(G + 1):
                    sp.wait_ge(s_mr, G + 2)
                    store_max_rows(k + 1)

            groups(sp, group)

        @block.gpsimd
        def _(pool):
            nc.gpsimd.memset(f32(mfull[:]), 0.0).then_inc(s_init, 1)
            nc.gpsimd.memset(v[:, :, :, DK:VW], 1.0).then_inc(s_init, 1)
            ch = Chain(pool, s_pool)
            for b in range(1, NB):
                pool.wait_ge(s_rope[b - 1], 16)
                pool.wait_ge(s_raw, b)
                ch.link(nc.gpsimd.tensor_tensor(raw, raw, rope[b - 1], ALU.mult))
                nc.gpsimd.tensor_tensor(raw[:, 0, :], raw[:, 0, :], raw[:, 1, :], ALU.add).then_inc(s_rot, 1)
                pool.wait_ge(s_rh, b)
                if b > 1:
                    pool.wait_ge(s_rp, (b - 1) * NG)
                nc.gpsimd.tensor_tensor(rot_lo[:], raw[:, 0, :], f32(rot_hi[:]), ALU.subtract).then_inc(s_rl, 1)

        @block.scalar
        def _(act):
            def copy_max_rows(G, bank):
                wait(act, s_mt, G + 1)
                wait(act, s_mrow, G * 64)
                nc.scalar.copy(mrows[:], ring[:, bank, :]).then_inc(s_mr, 1)

            def copy_acc(G):
                wait(act, s_pv, G * STEPS + STEPS)
                nc.scalar.copy(acc_s[:], acc[:]).then_inc(s_accs, 1)

            def prologue_work(u):
                if (t := beside(u, "v")) is not None and t % TPB == TPB - 1:
                    b = t // TPB
                    act.wait_ge(s_vp, b + 1)
                    nc.scalar.copy(v[:, b * TPB:(b + 1) * TPB, :, 0:DK].rearrange("p t h d -> p (t h) d"),
                                   acc[:].rearrange("p (n d) -> p n d", d=DK)).then_inc(s_ve, 1)
                if (b := beside(u, "raw")) is not None:
                    act.wait_ge(s_qpj, b)
                    if b > 1:
                        act.wait_ge(s_rl, b - 1)
                    nc.scalar.copy(raw, st_ps[:, 1, :].rearrange("p (m c) -> p m c", c=BLK)).then_inc(s_raw, 1)
                if (b := beside(u, "high")) is not None:
                    act.wait_ge(s_rot, b)
                    if b > 1:
                        act.wait_ge(s_rp, (b - 1) * NG)
                    nc.scalar.copy(rot_hi[:], raw[:, 0, :]).then_inc(s_rh, 1)
                if (n := beside(u, "row")) is not None:
                    act.wait_ge(s_rp, n + 1)
                    if n >= 2:
                        act.wait_ge(s_qst[n % 2], 16 * (n // 2))
                    nc.scalar.copy(qs[n % 2][:].bitcast(F32R), st_ps[:, 0, n % 2 * BLK:(n % 2 + 1) * BLK]).then_inc(s_ev, 1)

            for u in range(MU):
                prologue_work(u)
            copy_max_rows(0, (PROLOGUE.index(("rows", 0, 0)) - len(PROLOGUE)) % RING)

            def group(G, k, it):
                for s in range(STEPS):
                    T = G * STEPS + s
                    if s == 1 and k:
                        copy_acc(G - 1)
                    for pair in range(2):
                        if s == 14 and pair == 0 and exists(G + 1):
                            copy_max_rows(G + 1, place(("rows", 1, 0)) % RING)
                        act.wait_ge(s_st, T * 2 + pair + 1)
                        wait(act, s_pv, T - 1)
                        nc.scalar.activation(probs[:, 2 * (s % 2) + pair, :], st_ps[:, pair, :], ACT.Exp,
                                             scale=SCALE).then_inc(s_exp, 1)

            groups(act, group)
            nc.scalar.activation(warm[:], ident[:, 0:1], ACT.Sqrt)
            copy_acc(NGR - 1)

        @block.vector
        def _(dve):
            def reduce_max(G, k, u, bank):
                V = G * MU + u
                if u == 0:
                    wait(dve, s_mm, G * 3 - 3)
                dve.wait_ge(s_mx, V + 1)
                nc.vector.tensor_reduce(mpart[:, k % 2, u // CHUNKS, u % CHUNKS:u % CHUNKS + 1], ring[:, bank, :], AX_X, ALU.max).then_inc(s_red, 1)

            def negate_max(G, k):
                dve.wait_ge(s_red, G * MU + MU)
                nc.vector.tensor_reduce(mx[:], mpart[:, k % 2], AX_X, ALU.max).then_inc(s_mm, 1)
                dve.wait_ge(s_mm, G * 3 + 1)
                wait(dve, s_mt, G)
                mf = mfull[:].rearrange("p t (h r) -> p t h r", r=QUAD)
                mq = mx[:].rearrange("p (h t) -> p t h", t=TPB)
                if isinstance(G, int) and G == 0:
                    dve.wait_ge(s_init, 2)
                nc.vector.tensor_scalar(mf[:, :, :, ROW_M], mq, -1.0, None, ALU.mult).then_inc(s_mm, 1)
                dve.wait_ge(s_mm, G * 3 + 2)
                nc.vector.scalar_tensor_tensor(out=mf[:, :, :, ROW_M + 1], in0=mq, scalar=-1.0,
                                               in1=f32(mfull[:]).rearrange("p t (h r) -> p t h r", r=QUAD)[:, :, :, ROW_M],
                                               op0=ALU.mult, op1=ALU.subtract).then_inc(s_mm, 1)

            def normalize(G, k, it):
                b, g = it + k // NG, k % NG
                dve.wait_ge(s_at, G + 1)
                m4 = ring[:, place(("acc", -1, 0)) % RING, :].rearrange("p (t h r) -> p t h r", t=TPB, r=QUAD)
                nc.vector.reciprocal(rden[:], m4[:, :, :, DK]).then_inc(s_rd, 1)
                dve.wait_ge(s_rd, G + 1)
                tiles = slice(b * TPB, (b + 1) * TPB) if isinstance(b, int) else bass.ds(b * TPB, TPB)
                out = o_all[:, tiles, g * HG * DK:(g + 1) * HG * DK].rearrange("p t (h d) -> p t h d", d=DK)
                nc.vector.tensor_tensor(out, m4[:, :, :, 0:DK], rden[:].unsqueeze(3).to_broadcast([P, TPB, HG, DK]),
                                        ALU.mult).then_inc(s_o, 1)

            ch = Chain(dve, s_dve)

            def finish_block(b):
                dve.wait_ge(s_ot, b + 1)
                nc.vector.tensor_copy(oT[:], ring[:, O_BANK, :]).then_inc(s_oc, 1)
                if b == 0:
                    dve.wait_ge(s_in, 32)
                xs = x_tok[:, b * TPB:(b + 1) * TPB, :]
                ch.link(nc.vector.tensor_tensor(xs, xs, wob[:].unsqueeze(1).to_broadcast([P, TPB, DIM]), ALU.add))
                dve.wait_ge(s_pr, b + 1)
                ch.link(nc.vector.tensor_tensor(xs, xs, ring[:, X_BANK, :].rearrange("p (t d) -> p t d", d=DIM), ALU.add))
                block_stats(nc, ch, x_tok, st, mv, b)

            for n, (kind, G, u) in enumerate(PROLOGUE, -len(PROLOGUE)):
                if kind == "max":
                    reduce_max(G, G, u, n % RING)
                    if (G, u) == (0, MU - 1):
                        negate_max(0, 0)
                        dve.wait_ge(s_ve, NB)
                        nc.vector.memset(acc[:], 0.0).then_inc(s_init, 1)

            def group(G, k, it):
                for s in range(STEPS):
                    for item in WINDOW[s]:
                        kind, ahead, u = item
                        if kind == "acc" and k:
                            normalize(G - 1, k - 1, it)
                        elif kind == "max" and exists(G + ahead):
                            reduce_max(G + ahead, k + ahead, u, place(item) % RING)
                            if u == MU - 1:
                                negate_max(G + 1, k + 1)
                    if isinstance(G, int) and G == NGR - 1 and (s - 5) % 3 == 0 and 0 <= s - 5 < 9:
                        finish_block((s - 5) // 3)

            groups(dve, group)
            normalize(NGR - 1, NG - 1, NB - 1)
            finish_block(NB - 1)

        @block.tensor
        def _(pe):
            def bank_free(G, n):
                while True:
                    n -= RING
                    if isinstance(G, int) and G * len(FLAT) + n < 0:
                        if n < -len(PROLOGUE):
                            return
                        kind, ahead, u = PROLOGUE[n]
                    else:
                        kind, ahead, u = FLAT[n % len(FLAT)]
                        ahead += n // len(FLAT)
                    if exists(G + ahead):
                        break
                if kind == "max":
                    pe.wait_ge(s_red, (G + ahead) * MU + u + 1)
                elif kind == "rows":
                    pe.wait_ge(s_mr, G + ahead + 1)
                else:
                    wait(pe, s_o, G + ahead + 1)

            def max_scores(G, k, it, u, bank):
                V, g = G * MU + u, k % NG
                h, t, c = u // (TPB * CHUNKS), u // CHUNKS % TPB, u % CHUNKS
                if u == 0:
                    pe.wait_ge(s_qm[g], 64 * (it + k // NG + 1))
                nc.tensor.matmul(ring[:, bank, :], qm[g][:, h, t * P:(t + 1) * P],
                                 kr[:, g, c * BLK:(c + 1) * BLK], start=True, stop=True).then_inc(s_mx, 1)

            def transpose_max(G, bank):
                pe.wait_ge(s_mm, G * 3 + 3)
                for t in range(TPB):
                    mm = nc.tensor.matmul(ring[:, bank, t * P:(t + 1) * P], mfull[:, t, :], identr[:], start=True, stop=True)
                mm.then_inc(s_mt, 1)

            def transpose_acc(G, bank):
                pe.wait_ge(s_accs, G + 1)
                for t in range(TPB):
                    mm = nc.tensor.transpose(ring[:, bank, t * P:(t + 1) * P], acc_s[:, t * P:(t + 1) * P], ident[:])
                mm.then_inc(s_at, 1)

            def scores(G, k, s, head):
                T, g, pair = G * STEPS + s, k % NG, head // 2
                if head % 2 == 0:
                    wait(pe, s_exp, T * 2 + pair - 1)
                mm = nc.tensor.matmul(st_ps[:, pair, head % 2 * BLK:(head % 2 + 1) * BLK], kr[:, g, s * P:(s + 1) * P],
                                      qm[g][:, head, :], start=True, stop=True)
                if head % 2:
                    mm.then_inc(s_st, 1)

            def values(G, k, s):
                g = k % NG
                pe.wait_ge(s_exp, G * 2 * STEPS + 2 * s + 2)
                if s == 0:
                    wait(pe, s_accs, G)
                for h in range(HG):
                    mm = nc.tensor.matmul(acc[QUAD * h:QUAD * h + VW, :], v[:, s, g * HG + h, :],
                                          probs[:, 2 * (s % 2) + h // 2, (h % 2) * BLK:(h % 2 + 1) * BLK],
                                          start=(s == 0), stop=(s == STEPS - 1), skip_group_check=True)
                mm.then_inc(s_pv, 1)

            def project_values(t):
                at = t % TPB * P
                if t % TPB == 0:
                    wait(pe, s_ve, t // TPB)
                mm = nc.tensor.matmul(acc[:, at:at + P], hT[:, t * P:(t + 1) * P], wv[:],
                                      start=True, stop=True)
                if t % TPB == TPB - 1:
                    mm.then_inc(s_vp, 1)

            def project_queries(n):
                b, m, half = n // 4 + 1, n % 4 // 2, n % 2
                if n % 4 == 0:
                    wait(pe, s_raw, b - 1)
                at = half * BLK // 2
                mm = nc.tensor.matmul(st_ps[:, 1, m * BLK + at:m * BLK + at + BLK // 2], wqk[:, m * DIM:(m + 1) * DIM],
                                      hT[:, b * BLK + at:b * BLK + at + BLK // 2], start=True, stop=True)
                if n % 4 == 3:
                    mm.then_inc(s_qpj, 1)

            def replicate(n):
                pe.wait_ge(s_rl, n // NG + 1)
                wait(pe, s_ev, n - 1)
                bank = st_ps[:, 0, n % 2 * BLK:(n % 2 + 1) * BLK]
                w = slice(n % NG * P, (n % NG + 1) * P)
                nc.tensor.matmul(bank, sel[:, 0, w], rot_hi[:], start=True, stop=False)
                nc.tensor.matmul(bank, sel[:, 1, w], rot_lo[:], start=False, stop=True).then_inc(s_rp, 1)

            for n, (kind, G, u) in enumerate(PROLOGUE, -len(PROLOGUE)):
                bank_free(0, n)
                if kind == "max" and G == 0:
                    if beside(u, "v") is not None:
                        project_values(beside(u, "v"))
                    if beside(u, "project") is not None:
                        project_queries(beside(u, "project"))
                    if beside(u, "row") is not None:
                        replicate(beside(u, "row"))
                if kind == "rows":
                    transpose_max(0, n % RING)
                else:
                    max_scores(G, G, 0, u, n % RING)
            pe.wait_ge(s_init, 3)
            pe.wait_ge(s_ve, NB)
            pe.wait_ge(s_ev, (NB - 1) * NG)

            def group(G, k, it):
                for s in range(STEPS):
                    if s == 0:
                        pe.wait_ge(s_mrow, G * 64 + 64)
                    units = []
                    for item in WINDOW[s]:
                        kind, ahead, u = item
                        n = place(item)
                        if not exists(G + ahead) or (kind == "acc" and k == 0):
                            continue
                        if kind == "max":
                            units.append((ahead, u, n))
                            continue
                        bank_free(G, n)
                        if kind == "acc":
                            transpose_acc(G - 1, n % RING)
                        else:
                            transpose_max(G + 1, n % RING)
                    for head in range(HG):
                        scores(G, k, s, head)
                        for ahead, u, n in units[head:head + 1]:
                            bank_free(G, n)
                            max_scores(G + ahead, k + ahead, it, u, n % RING)
                    if s:
                        values(G, k, s - 1)
                    elif k:
                        values(G - 1, k - 1, STEPS - 1)
                    if isinstance(G, int) and G == NGR - 1 and 4 <= s < 13:
                        if (s - 4) % 3 == 0:
                            transpose_o((s - 4) // 3)
                        if (s - 4) % 3 == 1:
                            project_out((s - 4) // 3)

            def transpose_o(b):
                pe.wait_ge(s_o, (b + 1) * NG)
                if b == 0:
                    pe.wait_ge(s_in, 32)
                transpose_block(nc, ring[:, O_BANK, :], o_all, b, ident, s_ot)

            def project_out(b):
                pe.wait_ge(s_oc, b + 1)
                for t in range(TPB):
                    mm = nc.tensor.matmul(ring[:, X_BANK, t * P:(t + 1) * P], oT[:, t * P:(t + 1) * P], wo[:],
                                          start=True, stop=True)
                mm.then_inc(s_pr, 1)

            groups(pe, group)
            values(NGR - 1, NG - 1, STEPS - 1)
            bank_free(NGR, place(("acc", -1, 0)))
            transpose_acc(NGR - 1, place(("acc", -1, 0)) % RING)
            transpose_o(NB - 1)
            project_out(NB - 1)


def macaron_kernel(nc, dram):
    with ExitStack() as ctx:
        def sb(name, shape, dt=F32):
            return ctx.enter_context(nc.sbuf_tensor(name, shape, dt))

        x_tok = sb("x_tok", [P, NT, DIM])
        w1h, w1l = sb("w1h", [P, E * INNER], F32R), sb("w1l", [P, E * INNER], F32R)
        w2h, w2l = sb("w2h", [P, E * INNER], F32R), sb("w2l", [P, E * INNER], F32R)
        b2h, b2l = sb("b2h", [P, DIM], F32R), sb("b2l", [P, DIM], F32R)
        rw2 = sb("rw2", [P, P], F32R)
        consts = {
            "ident": sb("ident", [P, P]), "identr": sb("identr", [P, P], F32R),
            "onehot": sb("onehot", [P, E * P], F32R), "b1": sb("b1", [P, E * HALVES]), "rb": sb("rb", [2 * E, 1]),
        }
        weights = (w1h, w1l, w2h, w2l, b2h, b2l, rw2)
        st, mv = sb("st", [P, NT, 6]), sb("mv", [P, NT, 2])
        wqk, wv = sb("wqk", [P, 4 * DIM]), sb("wv", [P, DIM])
        c_scratch = [nc.dram_tensor(f"c_scratch{n}", [NB, E, BLK], F32, kind="Internal").ap() for n in range(2)]
        q_scratch = nc.dram_tensor("q_scratch", [NB, NG, P, BLK], F32, kind="Internal").ap()
        ffn_phase(nc, "f1_", dram, consts, x_tok, st, mv, weights, c_scratch[0], first=True, ahead=(wqk, wv))
        with ExitStack() as kv:
            kr = kv.enter_context(nc.sbuf_tensor("kr", [P, NG, SEQ], F32R))
            hT = kv.enter_context(nc.sbuf_tensor("hT", [P, SEQ], F32))
            sel = kv.enter_context(nc.sbuf_tensor("sel", [P, 4, NG * P], F32R))
            qm = [kv.enter_context(nc.sbuf_tensor(f"qm{g}", [P, HG, BLK], F32R)) for g in range(NG)]
            s_qm = [kv.enter_context(nc.semaphore(f"queries_loaded{g}")) for g in range(NG)]
            project_phase(nc, dram, consts, x_tok, mv, kr, hT, wqk, sel, qm, s_qm, q_scratch)
            attention_phase(nc, dram, consts, x_tok, st, mv, kr, hT, wqk, wv, sel, qm, s_qm, q_scratch)
        ffn_phase(nc, "f2_", dram, consts, x_tok, st, mv, weights, c_scratch[1], first=False)


def shape_constants(np):
    even, odd = np.arange(0, DIM, 2), np.arange(1, DIM, 2)
    pos = np.arange(SEQ, dtype=np.float32)
    freqs = np.exp(np.arange(0, DIM, 2, dtype=np.float32) * np.float32(-np.log(10000.0) / DIM)).astype(np.float32)
    ang = (freqs[:, None] * pos[None, :]).astype(np.float32)
    cos, sin = np.cos(ang), np.sin(ang)
    rope = np.stack([np.concatenate([cos, cos]), np.concatenate([-sin, sin])], axis=1).astype(np.float32)
    onehot = np.zeros((2 * E, E, P), np.float32)
    for e in range(E):
        onehot[e, e] = onehot[E + e, e] = 1.0
    sel = np.zeros((P, 4, NG, HG, QUAD), np.float32)
    rows = ((0, 2), (1,), (0, 1), (2,))
    for f, thirds in enumerate(rows):
        for third in thirds:
            for g in range(NG):
                for h in range(HG):
                    for d in range(DK):
                        sel[(g * HG + h) * DK + d, f, g, h, third * DK + d] = 1.0
    ones_rows = np.zeros((HG, QUAD), np.float32)
    ones_rows[:, ROW_M:ROW_M + 2] = 1.0
    return {"rope": rope, "onehot": onehot.reshape(2 * E, E * P), "sel": sel.reshape(P, 4, NG * P),
            "ones_rows": ones_rows.reshape(P, 1), "ident": np.eye(P, dtype=np.float32),
            "perm_a": np.concatenate([even, odd]), "perm_b": np.concatenate([odd, even])}


def kernel(L0_attn_x, L0_attn_wq, L0_attn_wk, L0_attn_wv, L0_attn_wo_w, L0_attn_wo_b, L0_ffn_router_w,
           L0_ffn_router_b, L0_ffn_w1, L0_ffn_b1, L0_ffn_w2, L0_ffn_b2):
    import numpy as np
    import concourse.bacc as bacc
    from concourse.bass_utils import run_bass_kernel_spmd

    c = shape_constants(np)
    pa, pb = c.pop("perm_a"), c.pop("perm_b")
    wq, wk = np.asarray(L0_attn_wq), np.asarray(L0_attn_wk)
    arrays = {
        "x": np.asarray(L0_attn_x).reshape(SEQ, DIM),
        "wqk": np.concatenate([wq[pa].T, wq[pb].T, wk[pa].T, wk[pb].T], axis=1),
        "wv": np.asarray(L0_attn_wv).T, "wo": np.asarray(L0_attn_wo_w).T,
        "wob": np.broadcast_to(np.asarray(L0_attn_wo_b), (P, DIM)),
        "rw": np.asarray(L0_ffn_router_w), "rb": np.concatenate([np.asarray(L0_ffn_router_b), np.zeros(E, np.float32)]).reshape(2 * E, 1),
        "w1": np.asarray(L0_ffn_w1), "w2": np.asarray(L0_ffn_w2),
        "b1": np.asarray(L0_ffn_b1).reshape(E, HALVES, P).transpose(2, 0, 1).reshape(P, E * HALVES),
        "b2": np.concatenate([np.asarray(L0_ffn_b2)] * 2 + [np.zeros((P - 2 * E, DIM), np.float32)], axis=0),
        **c,
    }
    arrays = {n: np.ascontiguousarray(a) for n, a in arrays.items()}
    nc = bacc.Bacc("TRN2", target_bir_lowering=False, num_devices=1)
    dram = {n: nc.dram_tensor("in_" + n, a.shape, F32, kind="ExternalInput").ap() for n, a in arrays.items()}
    dram["out"] = nc.dram_tensor("out", (SEQ, DIM), F32, kind="ExternalOutput").ap()
    macaron_kernel(nc, dram)
    r = run_bass_kernel_spmd(nc, [{"in_" + n: a for n, a in arrays.items()}], core_ids=[0])
    return r.results[0]["out"].reshape(1, SEQ, DIM)
```
